# Optimizing a Trainium2 kernel written in Bass

```python
import numpy as np
import jax
import jax.numpy as jnp

def _softmax(x, axis=-1):
    return jax.nn.softmax(x, axis=axis)

def _gelu(x):
    return jax.nn.gelu(x, approximate=True)

def _silu(x):
    return jax.nn.silu(x)

def _sigmoid(x):
    return jax.nn.sigmoid(x)

def _layernorm(x, axis=-1, eps=1e-05):
    m = jnp.mean(x, axis=axis, keepdims=True)
    v = jnp.var(x, axis=axis, keepdims=True)
    return (x - m) / jnp.sqrt(v + eps)

def _scatter_add(tgt, idx, src, axis=0):
    return tgt.at[idx].add(src)

def _segment_sum(src, seg, n):
    return jax.ops.segment_sum(src, seg, n)
kernel_name = 'mk_pixart_seq_d4_seqx_r4_4a2764'

def setup_inputs(seed: int=0):
    np.random.seed(seed)
    _w = jnp.asarray

    def _rec_inputs():
        import jax
        import jax.numpy as jnp
        _rk = jax.random.key(seed)
        x = -0.0002928 + 1 * jax.random.normal(jax.random.fold_in(_rk, 1), (2, 1024, 256), jnp.float32)
        _lenS = 1024 - jax.random.randint(jax.random.fold_in(_rk, 7), (2,), 0, max(1, 1024 // 4) + 1, jnp.int32)
        _lenS2 = 77 - jax.random.randint(jax.random.fold_in(_rk, 8), (2,), 0, max(1, 77 // 4) + 1, jnp.int32)
        cond_1024 = 0.000887014 + 1.03683 * jax.random.normal(jax.random.fold_in(_rk, 11), (2, 256), jnp.float32)
        _ctx_1024P = jax.random.normal(jax.random.fold_in(_rk, 12), (2, 16, 256), jnp.float32)
        _ctx_1024c = jax.random.dirichlet(jax.random.fold_in(_rk, 512), 0.3 * jnp.ones((16,), jnp.float32), (2, 77))
        _ctx_1024t = jnp.einsum('bsk,bkd->bsd', _ctx_1024c, _ctx_1024P)
        _ctx_1024t = _ctx_1024t * jax.lax.rsqrt(jnp.mean(jnp.square(_ctx_1024t)) + 1e-12) * 0.953939
        ctx_1024 = -0.00606593 + 0.997213 * (_ctx_1024t + 0.3 * jax.random.normal(jax.random.fold_in(_rk, 612), (2, 77, 256), jnp.float32))
        _validS = jnp.arange(1024)[None, :] < _lenS[:, None]
        _validS2 = jnp.arange(77)[None, :] < _lenS2[:, None]
        _causal = jnp.tril(jnp.ones((1024, 1024), dtype=bool))
        mask_BxS2_bf1 = jnp.ones((2, 77), dtype=bool)
        mask_SxS_bk0 = jnp.logical_not(jnp.broadcast_to(_validS[0:1, :], (1024, 1024)))
        return (x, cond_1024, ctx_1024, mask_BxS2_bf1, mask_SxS_bk0)
    x, cond_1024, ctx_1024, mask_BxS2_bf1, mask_SxS_bk0 = _rec_inputs()

    def _L0_xcond_setup():
        import jax, jax.numpy as jnp
        import numpy as np
        B, N, D, H, LC = (2, 256, 256, 16, 77)
        HD = D // H
        BLOCK = 16
        ROPE_BASE = 10000.0
        EPS = 1e-05

        def _block_diff_mask(n, block_size):
            idx = np.arange(2 * n)
            q = idx[:, None]
            kv = idx[None, :]
            fq = q >= n
            fkv = kv >= n
            bq = np.where(fq, (q - n) // block_size, q // block_size)
            bkv = np.where(fkv, (kv - n) // block_size, kv // block_size)
            block_diagonal = (bq == bkv) & (fq == fkv)
            offset_block_causal = (bq > bkv) & fkv & ~fq
            block_causal = (bq >= bkv) & fq & fkv
            return jnp.asarray(block_diagonal | offset_block_causal | block_causal)

        def _rope_tables(n):
            inv_freq = 1.0 / ROPE_BASE ** (np.arange(0, HD, 2, dtype=np.float32) / HD)
            freqs = np.outer(np.arange(n, dtype=np.float32), inv_freq)
            emb = np.concatenate([freqs, freqs], axis=-1)
            cos = jnp.asarray(np.cos(emb), jnp.float32)[None, :, None, :]
            sin = jnp.asarray(np.sin(emb), jnp.float32)[None, :, None, :]
            return (cos, sin)

        def _ln(x, w):
            xf = x.astype(jnp.float32)
            mu = jnp.mean(xf, axis=-1, keepdims=True)
            var = jnp.mean(jnp.square(xf - mu), axis=-1, keepdims=True)
            y = (xf - mu) * jax.lax.rsqrt(var + EPS)
            return y * w[None, None, :]

        def _apply_rope(t, cos, sin):
            t1, t2 = jnp.split(t, 2, axis=-1)
            rot = jnp.concatenate([-t2, t1], axis=-1)
            return t * cos + rot * sin

        def _attn(q, k, v, mask):
            scale = 1.0 / np.sqrt(HD)
            s = jnp.einsum('bqhd,bkhd->bhqk', q, k) * scale
            s = jnp.where(mask, s, jnp.finfo(s.dtype).min)
            a = jax.nn.softmax(s, axis=-1)
            return jnp.einsum('bhqk,bkhd->bqhd', a, v)
        key = jax.random.key(seed)
        ks = jax.random.split(key, 16)
        w = lambda k, shp: jax.random.normal(k, shp, jnp.float32) * 0.02
        inp = {'x': jax.random.normal(ks[0], (B, 2 * N, D), jnp.float32), 'cond_global': jax.random.normal(ks[1], (B, D), jnp.float32), 'cond_tokens': jax.random.normal(ks[2], (B, LC, D), jnp.float32), 'adaLN_W': w(ks[3], (D, 9 * D)), 'adaLN_b': w(ks[4], (9 * D,)), 'norm1_w': jnp.ones((D,), jnp.float32), 'qkv_W': w(ks[5], (D, 3 * D)), 'attn_out_W': w(ks[6], (D, D)), 'normc_w': jnp.ones((D,), jnp.float32), 'cq_W': w(ks[7], (D, D)), 'ck_W': w(ks[8], (D, D)), 'cv_W': w(ks[9], (D, D)), 'co_W': w(ks[10], (D, D)), 'norm2_w': jnp.ones((D,), jnp.float32), 'mlp_W1': w(ks[11], (D, 4 * D)), 'mlp_b1': w(ks[12], (4 * D,)), 'mlp_W2': w(ks[13], (4 * D, D)), 'mlp_b2': w(ks[14], (D,)), 'cond_kv_mask': jnp.ones((B, LC), bool), 'attn_mask': _block_diff_mask(N, BLOCK)}
        return inp
    _L0_xcond_all = _L0_xcond_setup()
    _L0_xcond_in = {k: v for k, v in _L0_xcond_all.items() if k in ('adaLN_W', 'adaLN_b', 'norm1_w', 'qkv_W', 'attn_out_W', 'normc_w', 'cq_W', 'ck_W', 'cv_W', 'co_W', 'norm2_w', 'mlp_W1', 'mlp_b1', 'mlp_W2', 'mlp_b2')}
    del _L0_xcond_all

    def _L1_xcond_setup():
        import jax, jax.numpy as jnp
        import numpy as np
        LN_EPS = 1e-06

        def _ln(x):
            mu = jnp.mean(x, axis=-1, keepdims=True)
            var = jnp.var(x, axis=-1, keepdims=True)
            return (x - mu) * jax.lax.rsqrt(var + LN_EPS)
        key = jax.random.key(seed)
        H, NH = (256, 16)
        B, N, S = (4, 256, 77)
        MLP = int(H * 4.0)
        ks = jax.random.split(key, 20)
        s = 1.0 / np.sqrt(H)
        return {'x': jax.random.normal(ks[0], (B, N, H), jnp.float32), 'c': jax.random.normal(ks[1], (B, H), jnp.float32), 'context': jax.random.normal(ks[2], (B, S, H), jnp.float32), 'W_mod': jax.random.normal(ks[3], (H, 6 * H), jnp.float32) * s, 'b_mod': jnp.zeros((6 * H,), jnp.float32), 'W_qkv': jax.random.normal(ks[4], (H, 3 * H), jnp.float32) * s, 'b_qkv': jnp.zeros((3 * H,), jnp.float32), 'W_proj': jax.random.normal(ks[5], (H, H), jnp.float32) * s, 'b_proj': jnp.zeros((H,), jnp.float32), 'W_qc': jax.random.normal(ks[6], (H, H), jnp.float32) * s, 'b_qc': jnp.zeros((H,), jnp.float32), 'W_kvc': jax.random.normal(ks[7], (H, 2 * H), jnp.float32) * s, 'b_kvc': jnp.zeros((2 * H,), jnp.float32), 'W_cproj': jax.random.normal(ks[8], (H, H), jnp.float32) * s, 'b_cproj': jnp.zeros((H,), jnp.float32), 'W_mlp1': jax.random.normal(ks[9], (H, MLP), jnp.float32) * s, 'b_mlp1': jnp.zeros((MLP,), jnp.float32), 'W_mlp2': jax.random.normal(ks[10], (MLP, H), jnp.float32) * (1.0 / np.sqrt(MLP)), 'b_mlp2': jnp.zeros((H,), jnp.float32)}
    _L1_xcond_all = _L1_xcond_setup()
    _L1_xcond_in = {k: v for k, v in _L1_xcond_all.items() if k in ('W_mod', 'b_mod', 'W_qkv', 'b_qkv', 'W_proj', 'b_proj', 'W_qc', 'b_qc', 'W_kvc', 'b_kvc', 'W_cproj', 'b_cproj', 'W_mlp1', 'b_mlp1', 'W_mlp2', 'b_mlp2')}
    del _L1_xcond_all

    def _L2_xcond_setup():
        import jax, jax.numpy as jnp
        import numpy as np
        C = 256
        H = 16
        D = C // H
        WIN = 128
        SHIFT = 64
        TOPK = 16
        HID = 1024
        EPS = 1e-06

        def _ln(x):
            x32 = x.astype(jnp.float32)
            m = x32.mean(-1, keepdims=True)
            v = jnp.mean((x32 - m) ** 2, axis=-1, keepdims=True)
            return ((x32 - m) * jax.lax.rsqrt(v + EPS)).astype(x.dtype)

        def _self_attn(h, w_qkv, b_qkv, w_so, b_so):
            B, L, _ = h.shape
            qkv = h @ w_qkv + b_qkv
            qkv = jnp.roll(qkv, -SHIFT, axis=1)
            nw = L // WIN
            qkv = qkv.reshape(B, nw, WIN, 3, H, D)
            q, k, v = (qkv[:, :, :, 0], qkv[:, :, :, 1], qkv[:, :, :, 2])
            scores = jnp.einsum('bnqhd,bnkhd->bnhqk', q, k) / jnp.sqrt(jnp.float32(D)).astype(h.dtype)
            attn = jax.nn.softmax(scores, axis=-1)
            o = jnp.einsum('bnhqk,bnkhd->bnqhd', attn, v).reshape(B, L, C)
            o = jnp.roll(o, SHIFT, axis=1)
            return o @ w_so + b_so

        def _topk_cross_attn(h, ctx, w_q, b_q, w_kv, b_kv, w_co, b_co):
            B, L, _ = h.shape
            Lc = ctx.shape[1]
            q = (h @ w_q + b_q).reshape(B, L, H, D)
            kv = (ctx @ w_kv + b_kv).reshape(B, Lc, 2, H, D)
            k, v = (kv[:, :, 0], kv[:, :, 1])
            scores = jnp.einsum('bqhd,bkhd->bhqk', q, k) / jnp.sqrt(jnp.float32(D)).astype(h.dtype)
            top_s, top_i = jax.lax.top_k(scores, TOPK)
            attn = jax.nn.softmax(top_s, axis=-1)
            v_bh = jnp.transpose(v, (0, 2, 1, 3))
            vg = jnp.take_along_axis(v_bh[:, :, None, :, :], top_i[..., None], axis=3)
            o = jnp.einsum('bhqk,bhqkd->bqhd', attn, vg).reshape(B, L, C)
            return o @ w_co + b_co

        def _swiglu(h, w_m1, b_m1, w_m2, b_m2):
            u = h @ w_m1 + b_m1
            a, b = (u[..., :HID], u[..., HID:])
            return jax.nn.silu(a) * b @ w_m2 + b_m2
        key = jax.random.key(seed)
        ks = jax.random.split(key, 24)
        s = 0.02
        inp = {'x': jax.random.normal(ks[0], (2, 1024, C), jnp.float32), 'mod': jax.random.normal(ks[1], (2, C), jnp.float32), 'context': jax.random.normal(ks[2], (2, 256, C), jnp.float32), 'w_ada': jax.random.normal(ks[3], (C, 9 * C), jnp.float32) * s, 'b_ada': jnp.zeros((9 * C,), jnp.float32), 'w_qkv': jax.random.normal(ks[4], (C, 3 * C), jnp.float32) * s, 'b_qkv': jnp.zeros((3 * C,), jnp.float32), 'w_so': jax.random.normal(ks[5], (C, C), jnp.float32) * s, 'b_so': jnp.zeros((C,), jnp.float32), 'w_q': jax.random.normal(ks[6], (C, C), jnp.float32) * s, 'b_q': jnp.zeros((C,), jnp.float32), 'w_kv': jax.random.normal(ks[7], (C, 2 * C), jnp.float32) * s, 'b_kv': jnp.zeros((2 * C,), jnp.float32), 'w_co': jax.random.normal(ks[8], (C, C), jnp.float32) * s, 'b_co': jnp.zeros((C,), jnp.float32), 'w_m1': jax.random.normal(ks[9], (C, 2 * HID), jnp.float32) * s, 'b_m1': jnp.zeros((2 * HID,), jnp.float32), 'w_m2': jax.random.normal(ks[10], (HID, C), jnp.float32) * s, 'b_m2': jnp.zeros((C,), jnp.float32)}
        return inp
    _L2_xcond_all = _L2_xcond_setup()
    _L2_xcond_in = {k: v for k, v in _L2_xcond_all.items() if k in ('w_ada', 'b_ada', 'w_qkv', 'b_qkv', 'w_so', 'b_so', 'w_q', 'b_q', 'w_kv', 'b_kv', 'w_co', 'b_co', 'w_m1', 'b_m1', 'w_m2', 'b_m2')}
    del _L2_xcond_all

    def _L3_xcond_setup():
        import jax, jax.numpy as jnp
        import numpy as np
        import math
        D_MODEL = 256
        N_HEADS = 16
        HEAD_DIM = D_MODEL // N_HEADS
        D_FF = 1024
        EPS = 1e-05
        ROPE_BASE = 10000.0

        def _rope(t):
            L, Dh = (t.shape[1], t.shape[-1])
            half = Dh // 2
            inv_freq = 1.0 / ROPE_BASE ** (jnp.arange(half, dtype=t.dtype) / half)
            ang = jnp.arange(L, dtype=t.dtype)[:, None] * inv_freq[None, :]
            cos = jnp.cos(ang)[None, :, None, :]
            sin = jnp.sin(ang)[None, :, None, :]
            t1, t2 = (t[..., :half], t[..., half:])
            return jnp.concatenate([t1 * cos - t2 * sin, t2 * cos + t1 * sin], axis=-1)

        def _adaln(x, emb, w, b):
            e = emb[:, 0, :]
            gb = e @ w.T + b
            gamma, beta = jnp.split(gb, 2, axis=-1)
            mu = x.mean(-1, keepdims=True)
            var = x.var(-1, keepdims=True)
            xn = (x - mu) * jax.lax.rsqrt(var + EPS)
            return xn * (1.0 + gamma[:, None, :]) + beta[:, None, :]

        def _attn(q, k, v):
            scale = 1.0 / math.sqrt(HEAD_DIM)
            scores = jnp.einsum('bqhd,bkhd->bhqk', q, k) * scale
            w = jax.nn.softmax(scores, axis=-1)
            out = jnp.einsum('bhqk,bkhd->bqhd', w, v)
            B, Lq = (out.shape[0], out.shape[1])
            return out.reshape(B, Lq, D_MODEL)
        key = jax.random.key(seed)
        ks = jax.random.split(key, 24)
        s = 0.02
        inp = {'x': jax.random.normal(ks[0], (2, 512, D_MODEL), jnp.float32), 'noise_emb': jax.random.normal(ks[1], (2, 1, D_MODEL), jnp.float32), 'context': jax.random.normal(ks[2], (2, 256, D_MODEL), jnp.float32), 'ln1_w': jax.random.normal(ks[3], (2 * D_MODEL, D_MODEL), jnp.float32) * s, 'ln1_b': jax.random.normal(ks[4], (2 * D_MODEL,), jnp.float32) * s, 'ln2_w': jax.random.normal(ks[5], (2 * D_MODEL, D_MODEL), jnp.float32) * s, 'ln2_b': jax.random.normal(ks[6], (2 * D_MODEL,), jnp.float32) * s, 'ln3_w': jax.random.normal(ks[7], (2 * D_MODEL, D_MODEL), jnp.float32) * s, 'ln3_b': jax.random.normal(ks[8], (2 * D_MODEL,), jnp.float32) * s, 'qkv_w': jax.random.normal(ks[9], (3 * D_MODEL, D_MODEL), jnp.float32) * s, 'sa_out_w': jax.random.normal(ks[10], (D_MODEL, D_MODEL), jnp.float32) * s, 'q_w': jax.random.normal(ks[11], (D_MODEL, D_MODEL), jnp.float32) * s, 'k_w': jax.random.normal(ks[12], (D_MODEL, D_MODEL), jnp.float32) * s, 'v_w': jax.random.normal(ks[13], (D_MODEL, D_MODEL), jnp.float32) * s, 'ca_out_w': jax.random.normal(ks[14], (D_MODEL, D_MODEL), jnp.float32) * s, 'ffn_w1': jax.random.normal(ks[15], (D_FF, D_MODEL), jnp.float32) * s, 'ffn_b1': jax.random.normal(ks[16], (D_FF,), jnp.float32) * s, 'ffn_w2': jax.random.normal(ks[17], (D_MODEL, D_FF), jnp.float32) * s, 'ffn_b2': jax.random.normal(ks[18], (D_MODEL,), jnp.float32) * s}
        return inp
    _L3_xcond_all = _L3_xcond_setup()
    _L3_xcond_in = {k: v for k, v in _L3_xcond_all.items() if k in ('ln1_w', 'ln1_b', 'ln2_w', 'ln2_b', 'ln3_w', 'ln3_b', 'qkv_w', 'sa_out_w', 'q_w', 'k_w', 'v_w', 'ca_out_w', 'ffn_w1', 'ffn_b1', 'ffn_w2', 'ffn_b2')}
    del _L3_xcond_all
    return {'x': x, 'cond_1024': cond_1024, 'ctx_1024': ctx_1024, 'mask_BxS2_bf1': mask_BxS2_bf1, 'mask_SxS_bk0': mask_SxS_bk0, 'L0_xcond_adaLN_W': _L0_xcond_in['adaLN_W'], 'L0_xcond_adaLN_b': _L0_xcond_in['adaLN_b'], 'L0_xcond_norm1_w': _L0_xcond_in['norm1_w'], 'L0_xcond_qkv_W': _L0_xcond_in['qkv_W'], 'L0_xcond_attn_out_W': _L0_xcond_in['attn_out_W'], 'L0_xcond_normc_w': _L0_xcond_in['normc_w'], 'L0_xcond_cq_W': _L0_xcond_in['cq_W'], 'L0_xcond_ck_W': _L0_xcond_in['ck_W'], 'L0_xcond_cv_W': _L0_xcond_in['cv_W'], 'L0_xcond_co_W': _L0_xcond_in['co_W'], 'L0_xcond_norm2_w': _L0_xcond_in['norm2_w'], 'L0_xcond_mlp_W1': _L0_xcond_in['mlp_W1'], 'L0_xcond_mlp_b1': _L0_xcond_in['mlp_b1'], 'L0_xcond_mlp_W2': _L0_xcond_in['mlp_W2'], 'L0_xcond_mlp_b2': _L0_xcond_in['mlp_b2'], 'L1_xcond_W_mod': _L1_xcond_in['W_mod'], 'L1_xcond_b_mod': _L1_xcond_in['b_mod'], 'L1_xcond_W_qkv': _L1_xcond_in['W_qkv'], 'L1_xcond_b_qkv': _L1_xcond_in['b_qkv'], 'L1_xcond_W_proj': _L1_xcond_in['W_proj'], 'L1_xcond_b_proj': _L1_xcond_in['b_proj'], 'L1_xcond_W_qc': _L1_xcond_in['W_qc'], 'L1_xcond_b_qc': _L1_xcond_in['b_qc'], 'L1_xcond_W_kvc': _L1_xcond_in['W_kvc'], 'L1_xcond_b_kvc': _L1_xcond_in['b_kvc'], 'L1_xcond_W_cproj': _L1_xcond_in['W_cproj'], 'L1_xcond_b_cproj': _L1_xcond_in['b_cproj'], 'L1_xcond_W_mlp1': _L1_xcond_in['W_mlp1'], 'L1_xcond_b_mlp1': _L1_xcond_in['b_mlp1'], 'L1_xcond_W_mlp2': _L1_xcond_in['W_mlp2'], 'L1_xcond_b_mlp2': _L1_xcond_in['b_mlp2'], 'L2_xcond_w_ada': _L2_xcond_in['w_ada'], 'L2_xcond_b_ada': _L2_xcond_in['b_ada'], 'L2_xcond_w_qkv': _L2_xcond_in['w_qkv'], 'L2_xcond_b_qkv': _L2_xcond_in['b_qkv'], 'L2_xcond_w_so': _L2_xcond_in['w_so'], 'L2_xcond_b_so': _L2_xcond_in['b_so'], 'L2_xcond_w_q': _L2_xcond_in['w_q'], 'L2_xcond_b_q': _L2_xcond_in['b_q'], 'L2_xcond_w_kv': _L2_xcond_in['w_kv'], 'L2_xcond_b_kv': _L2_xcond_in['b_kv'], 'L2_xcond_w_co': _L2_xcond_in['w_co'], 'L2_xcond_b_co': _L2_xcond_in['b_co'], 'L2_xcond_w_m1': _L2_xcond_in['w_m1'], 'L2_xcond_b_m1': _L2_xcond_in['b_m1'], 'L2_xcond_w_m2': _L2_xcond_in['w_m2'], 'L2_xcond_b_m2': _L2_xcond_in['b_m2'], 'L3_xcond_ln1_w': _L3_xcond_in['ln1_w'], 'L3_xcond_ln1_b': _L3_xcond_in['ln1_b'], 'L3_xcond_ln2_w': _L3_xcond_in['ln2_w'], 'L3_xcond_ln2_b': _L3_xcond_in['ln2_b'], 'L3_xcond_ln3_w': _L3_xcond_in['ln3_w'], 'L3_xcond_ln3_b': _L3_xcond_in['ln3_b'], 'L3_xcond_qkv_w': _L3_xcond_in['qkv_w'], 'L3_xcond_sa_out_w': _L3_xcond_in['sa_out_w'], 'L3_xcond_q_w': _L3_xcond_in['q_w'], 'L3_xcond_k_w': _L3_xcond_in['k_w'], 'L3_xcond_v_w': _L3_xcond_in['v_w'], 'L3_xcond_ca_out_w': _L3_xcond_in['ca_out_w'], 'L3_xcond_ffn_w1': _L3_xcond_in['ffn_w1'], 'L3_xcond_ffn_b1': _L3_xcond_in['ffn_b1'], 'L3_xcond_ffn_w2': _L3_xcond_in['ffn_w2'], 'L3_xcond_ffn_b2': _L3_xcond_in['ffn_b2']}

def reference(x, cond_1024, ctx_1024, mask_BxS2_bf1, mask_SxS_bk0, L0_xcond_adaLN_W, L0_xcond_adaLN_b, L0_xcond_norm1_w, L0_xcond_qkv_W, L0_xcond_attn_out_W, L0_xcond_normc_w, L0_xcond_cq_W, L0_xcond_ck_W, L0_xcond_cv_W, L0_xcond_co_W, L0_xcond_norm2_w, L0_xcond_mlp_W1, L0_xcond_mlp_b1, L0_xcond_mlp_W2, L0_xcond_mlp_b2, L1_xcond_W_mod, L1_xcond_b_mod, L1_xcond_W_qkv, L1_xcond_b_qkv, L1_xcond_W_proj, L1_xcond_b_proj, L1_xcond_W_qc, L1_xcond_b_qc, L1_xcond_W_kvc, L1_xcond_b_kvc, L1_xcond_W_cproj, L1_xcond_b_cproj, L1_xcond_W_mlp1, L1_xcond_b_mlp1, L1_xcond_W_mlp2, L1_xcond_b_mlp2, L2_xcond_w_ada, L2_xcond_b_ada, L2_xcond_w_qkv, L2_xcond_b_qkv, L2_xcond_w_so, L2_xcond_b_so, L2_xcond_w_q, L2_xcond_b_q, L2_xcond_w_kv, L2_xcond_b_kv, L2_xcond_w_co, L2_xcond_b_co, L2_xcond_w_m1, L2_xcond_b_m1, L2_xcond_w_m2, L2_xcond_b_m2, L3_xcond_ln1_w, L3_xcond_ln1_b, L3_xcond_ln2_w, L3_xcond_ln2_b, L3_xcond_ln3_w, L3_xcond_ln3_b, L3_xcond_qkv_w, L3_xcond_sa_out_w, L3_xcond_q_w, L3_xcond_k_w, L3_xcond_v_w, L3_xcond_ca_out_w, L3_xcond_ffn_w1, L3_xcond_ffn_b1, L3_xcond_ffn_w2, L3_xcond_ffn_b2):
    import jax
    import jax.numpy as jnp

    def _L0_xcond_ref(x, cond_global, cond_tokens, adaLN_W, adaLN_b, norm1_w, qkv_W, attn_out_W, normc_w, cq_W, ck_W, cv_W, co_W, norm2_w, mlp_W1, mlp_b1, mlp_W2, mlp_b2, cond_kv_mask, attn_mask):
        import jax, jax.numpy as jnp
        import numpy as np
        B, N, D, H, LC = (2, 256, 256, 16, 77)
        HD = D // H
        BLOCK = 16
        ROPE_BASE = 10000.0
        EPS = 1e-05

        def _block_diff_mask(n, block_size):
            idx = np.arange(2 * n)
            q = idx[:, None]
            kv = idx[None, :]
            fq = q >= n
            fkv = kv >= n
            bq = np.where(fq, (q - n) // block_size, q // block_size)
            bkv = np.where(fkv, (kv - n) // block_size, kv // block_size)
            block_diagonal = (bq == bkv) & (fq == fkv)
            offset_block_causal = (bq > bkv) & fkv & ~fq
            block_causal = (bq >= bkv) & fq & fkv
            return jnp.asarray(block_diagonal | offset_block_causal | block_causal)

        def _rope_tables(n):
            inv_freq = 1.0 / ROPE_BASE ** (np.arange(0, HD, 2, dtype=np.float32) / HD)
            freqs = np.outer(np.arange(n, dtype=np.float32), inv_freq)
            emb = np.concatenate([freqs, freqs], axis=-1)
            cos = jnp.asarray(np.cos(emb), jnp.float32)[None, :, None, :]
            sin = jnp.asarray(np.sin(emb), jnp.float32)[None, :, None, :]
            return (cos, sin)

        def _ln(x, w):
            xf = x.astype(jnp.float32)
            mu = jnp.mean(xf, axis=-1, keepdims=True)
            var = jnp.mean(jnp.square(xf - mu), axis=-1, keepdims=True)
            y = (xf - mu) * jax.lax.rsqrt(var + EPS)
            return y * w[None, None, :]

        def _apply_rope(t, cos, sin):
            t1, t2 = jnp.split(t, 2, axis=-1)
            rot = jnp.concatenate([-t2, t1], axis=-1)
            return t * cos + rot * sin

        def _attn(q, k, v, mask):
            scale = 1.0 / np.sqrt(HD)
            s = jnp.einsum('bqhd,bkhd->bhqk', q, k) * scale
            s = jnp.where(mask, s, jnp.finfo(s.dtype).min)
            a = jax.nn.softmax(s, axis=-1)
            return jnp.einsum('bhqk,bkhd->bqhd', a, v)
        b, s, d = x.shape
        n = s // 2
        mod = (cond_global @ adaLN_W + adaLN_b)[:, None, :]
        sh_msa, sc_msa, g_msa, sh_x, sc_x, g_x, sh_mlp, sc_mlp, g_mlp = jnp.split(mod, 9, axis=-1)
        x_norm = _ln(x, norm1_w) * (1 + sc_msa) + sh_msa
        cos, sin = _rope_tables(n)

        def qkv(h):
            t = (h @ qkv_W).reshape(b, n, 3, H, HD)
            q, k, v = (t[:, :, 0], t[:, :, 1], t[:, :, 2])
            return (_apply_rope(q, cos, sin), _apply_rope(k, cos, sin), v)
        q1, k1, v1 = qkv(x_norm[:, :n])
        q2, k2, v2 = qkv(x_norm[:, n:])
        q = jnp.concatenate([q1, q2], axis=1)
        k = jnp.concatenate([k1, k2], axis=1)
        v = jnp.concatenate([v1, v2], axis=1)
        self_out = _attn(q, k, v, attn_mask[None, None]).reshape(b, s, d) @ attn_out_W
        x = x + g_msa * self_out
        xc = _ln(x, normc_w) * (1 + sc_x) + sh_x
        qc = (xc @ cq_W).reshape(b, s, H, HD)
        kc = (cond_tokens @ ck_W).reshape(b, LC, H, HD)
        vc = (cond_tokens @ cv_W).reshape(b, LC, H, HD)
        cross = _attn(qc, kc, vc, cond_kv_mask[:, None, None, :]).reshape(b, s, d) @ co_W
        x = x + g_x * cross
        xm = _ln(x, norm2_w) * (1 + sc_mlp) + sh_mlp
        h = jax.nn.gelu(xm @ mlp_W1 + mlp_b1, approximate=True)
        mlp_out = h @ mlp_W2 + mlp_b2
        return x + g_mlp * mlp_out

    def _L1_xcond_ref(x, c, context, W_mod, b_mod, W_qkv, b_qkv, W_proj, b_proj, W_qc, b_qc, W_kvc, b_kvc, W_cproj, b_cproj, W_mlp1, b_mlp1, W_mlp2, b_mlp2):
        import jax, jax.numpy as jnp
        import numpy as np
        LN_EPS = 1e-06

        def _ln(x):
            mu = jnp.mean(x, axis=-1, keepdims=True)
            var = jnp.var(x, axis=-1, keepdims=True)
            return (x - mu) * jax.lax.rsqrt(var + LN_EPS)
        B, N, H = x.shape
        NH = 16
        hd = H // NH
        scale = hd ** (-0.5)
        c_proj = jax.nn.silu(c) @ W_mod + b_mod
        shift_a, scale_a, gate_a, shift_m, scale_m, gate_m = jnp.split(c_proj, 6, axis=-1)

        def modulate(t, shift, sc):
            return t * (1 + sc[:, None]) + shift[:, None]
        x_norm = modulate(_ln(x), shift_a, scale_a)
        qkv = x_norm @ W_qkv + b_qkv
        q, k, v = jnp.split(qkv, 3, axis=-1)
        q = q.reshape(B, N, NH, hd).transpose(0, 2, 1, 3)
        k = k.reshape(B, N, NH, hd).transpose(0, 2, 1, 3)
        v = v.reshape(B, N, NH, hd).transpose(0, 2, 1, 3)
        attn_w = jax.nn.softmax(jnp.einsum('bhqd,bhkd->bhqk', q, k) * scale, axis=-1)
        attn_out = jnp.einsum('bhqk,bhkd->bhqd', attn_w, v)
        attn_out = attn_out.transpose(0, 2, 1, 3).reshape(B, N, H)
        attn_out = attn_out @ W_proj + b_proj
        x = x + gate_a[:, None] * attn_out
        S = context.shape[1]
        q_c = _ln(x) @ W_qc + b_qc
        kv_c = _ln(context) @ W_kvc + b_kvc
        k_c, v_c = jnp.split(kv_c, 2, axis=-1)
        q_c = q_c.reshape(B, N, NH, hd).transpose(0, 2, 1, 3)
        k_c = k_c.reshape(B, S, NH, hd).transpose(0, 2, 1, 3)
        v_c = v_c.reshape(B, S, NH, hd).transpose(0, 2, 1, 3)
        c_attn_w = jax.nn.softmax(jnp.einsum('bhqd,bhsd->bhqs', q_c, k_c) * scale, axis=-1)
        c_attn_out = jnp.einsum('bhqs,bhsd->bhqd', c_attn_w, v_c)
        c_attn_out = c_attn_out.transpose(0, 2, 1, 3).reshape(B, N, H)
        c_attn_out = c_attn_out @ W_cproj + b_cproj
        x = x + c_attn_out
        x_norm2 = modulate(_ln(x), shift_m, scale_m)
        h = jax.nn.gelu(x_norm2 @ W_mlp1 + b_mlp1)
        h = h @ W_mlp2 + b_mlp2
        x = x + gate_m[:, None] * h
        return x

    def _L2_xcond_ref(x, mod, context, w_ada, b_ada, w_qkv, b_qkv, w_so, b_so, w_q, b_q, w_kv, b_kv, w_co, b_co, w_m1, b_m1, w_m2, b_m2):
        import jax, jax.numpy as jnp
        import numpy as np
        C = 256
        H = 16
        D = C // H
        WIN = 128
        SHIFT = 64
        TOPK = 16
        HID = 1024
        EPS = 1e-06

        def _ln(x):
            x32 = x.astype(jnp.float32)
            m = x32.mean(-1, keepdims=True)
            v = jnp.mean((x32 - m) ** 2, axis=-1, keepdims=True)
            return ((x32 - m) * jax.lax.rsqrt(v + EPS)).astype(x.dtype)

        def _self_attn(h, w_qkv, b_qkv, w_so, b_so):
            B, L, _ = h.shape
            qkv = h @ w_qkv + b_qkv
            qkv = jnp.roll(qkv, -SHIFT, axis=1)
            nw = L // WIN
            qkv = qkv.reshape(B, nw, WIN, 3, H, D)
            q, k, v = (qkv[:, :, :, 0], qkv[:, :, :, 1], qkv[:, :, :, 2])
            scores = jnp.einsum('bnqhd,bnkhd->bnhqk', q, k) / jnp.sqrt(jnp.float32(D)).astype(h.dtype)
            attn = jax.nn.softmax(scores, axis=-1)
            o = jnp.einsum('bnhqk,bnkhd->bnqhd', attn, v).reshape(B, L, C)
            o = jnp.roll(o, SHIFT, axis=1)
            return o @ w_so + b_so

        def _topk_cross_attn(h, ctx, w_q, b_q, w_kv, b_kv, w_co, b_co):
            B, L, _ = h.shape
            Lc = ctx.shape[1]
            q = (h @ w_q + b_q).reshape(B, L, H, D)
            kv = (ctx @ w_kv + b_kv).reshape(B, Lc, 2, H, D)
            k, v = (kv[:, :, 0], kv[:, :, 1])
            scores = jnp.einsum('bqhd,bkhd->bhqk', q, k) / jnp.sqrt(jnp.float32(D)).astype(h.dtype)
            top_s, top_i = jax.lax.top_k(scores, TOPK)
            attn = jax.nn.softmax(top_s, axis=-1)
            v_bh = jnp.transpose(v, (0, 2, 1, 3))
            vg = jnp.take_along_axis(v_bh[:, :, None, :, :], top_i[..., None], axis=3)
            o = jnp.einsum('bhqk,bhqkd->bqhd', attn, vg).reshape(B, L, C)
            return o @ w_co + b_co

        def _swiglu(h, w_m1, b_m1, w_m2, b_m2):
            u = h @ w_m1 + b_m1
            a, b = (u[..., :HID], u[..., HID:])
            return jax.nn.silu(a) * b @ w_m2 + b_m2
        m = jax.nn.silu(mod) @ w_ada + b_ada
        sh_msa, sc_msa, g_msa, sh_mca, sc_mca, g_mca, sh_mlp, sc_mlp, g_mlp = [m[:, i * C:(i + 1) * C][:, None, :] for i in range(9)]
        h = _ln(x) * (1 + sc_msa) + sh_msa
        h = _self_attn(h, w_qkv, b_qkv, w_so, b_so)
        x = x + h * g_msa
        h = _ln(x) * (1 + sc_mca) + sh_mca
        h = _topk_cross_attn(h, context, w_q, b_q, w_kv, b_kv, w_co, b_co)
        x = x + h * g_mca
        h = _ln(x) * (1 + sc_mlp) + sh_mlp
        h = _swiglu(h, w_m1, b_m1, w_m2, b_m2)
        x = x + h * g_mlp
        return x

    def _L3_xcond_ref(x, noise_emb, context, ln1_w, ln1_b, ln2_w, ln2_b, ln3_w, ln3_b, qkv_w, sa_out_w, q_w, k_w, v_w, ca_out_w, ffn_w1, ffn_b1, ffn_w2, ffn_b2):
        import jax, jax.numpy as jnp
        import numpy as np
        import math
        D_MODEL = 256
        N_HEADS = 16
        HEAD_DIM = D_MODEL // N_HEADS
        D_FF = 1024
        EPS = 1e-05
        ROPE_BASE = 10000.0

        def _rope(t):
            L, Dh = (t.shape[1], t.shape[-1])
            half = Dh // 2
            inv_freq = 1.0 / ROPE_BASE ** (jnp.arange(half, dtype=t.dtype) / half)
            ang = jnp.arange(L, dtype=t.dtype)[:, None] * inv_freq[None, :]
            cos = jnp.cos(ang)[None, :, None, :]
            sin = jnp.sin(ang)[None, :, None, :]
            t1, t2 = (t[..., :half], t[..., half:])
            return jnp.concatenate([t1 * cos - t2 * sin, t2 * cos + t1 * sin], axis=-1)

        def _adaln(x, emb, w, b):
            e = emb[:, 0, :]
            gb = e @ w.T + b
            gamma, beta = jnp.split(gb, 2, axis=-1)
            mu = x.mean(-1, keepdims=True)
            var = x.var(-1, keepdims=True)
            xn = (x - mu) * jax.lax.rsqrt(var + EPS)
            return xn * (1.0 + gamma[:, None, :]) + beta[:, None, :]

        def _attn(q, k, v):
            scale = 1.0 / math.sqrt(HEAD_DIM)
            scores = jnp.einsum('bqhd,bkhd->bhqk', q, k) * scale
            w = jax.nn.softmax(scores, axis=-1)
            out = jnp.einsum('bhqk,bkhd->bqhd', w, v)
            B, Lq = (out.shape[0], out.shape[1])
            return out.reshape(B, Lq, D_MODEL)
        B, L, D = x.shape
        L_ctx = context.shape[1]
        res = x
        xn = _adaln(x, noise_emb, ln1_w, ln1_b)
        qkv = xn @ qkv_w.T
        q, k, v = jnp.split(qkv, 3, axis=-1)
        q = _rope(q.reshape(B, L, N_HEADS, HEAD_DIM))
        k = _rope(k.reshape(B, L, N_HEADS, HEAD_DIM))
        v = v.reshape(B, L, N_HEADS, HEAD_DIM)
        sa = _attn(q, k, v) @ sa_out_w.T
        x = res + sa
        res = x
        xn = _adaln(x, noise_emb, ln2_w, ln2_b)
        q = _rope((xn @ q_w.T).reshape(B, L, N_HEADS, HEAD_DIM))
        k = _rope((context @ k_w.T).reshape(B, L_ctx, N_HEADS, HEAD_DIM))
        v = (context @ v_w.T).reshape(B, L_ctx, N_HEADS, HEAD_DIM)
        ca = _attn(q, k, v) @ ca_out_w.T
        x = res + ca
        res = x
        xn = _adaln(x, noise_emb, ln3_w, ln3_b)
        h = jax.nn.gelu(xn @ ffn_w1.T + ffn_b1, approximate=False)
        x = res + (h @ ffn_w2.T + ffn_b2)
        return x
    x = _L0_xcond_ref(x, cond_1024, ctx_1024, L0_xcond_adaLN_W, L0_xcond_adaLN_b, L0_xcond_norm1_w, L0_xcond_qkv_W, L0_xcond_attn_out_W, L0_xcond_normc_w, L0_xcond_cq_W, L0_xcond_ck_W, L0_xcond_cv_W, L0_xcond_co_W, L0_xcond_norm2_w, L0_xcond_mlp_W1, L0_xcond_mlp_b1, L0_xcond_mlp_W2, L0_xcond_mlp_b2, mask_BxS2_bf1, mask_SxS_bk0)
    x = _L1_xcond_ref(x, cond_1024, ctx_1024, L1_xcond_W_mod, L1_xcond_b_mod, L1_xcond_W_qkv, L1_xcond_b_qkv, L1_xcond_W_proj, L1_xcond_b_proj, L1_xcond_W_qc, L1_xcond_b_qc, L1_xcond_W_kvc, L1_xcond_b_kvc, L1_xcond_W_cproj, L1_xcond_b_cproj, L1_xcond_W_mlp1, L1_xcond_b_mlp1, L1_xcond_W_mlp2, L1_xcond_b_mlp2)
    x = _L2_xcond_ref(x, cond_1024, ctx_1024, L2_xcond_w_ada, L2_xcond_b_ada, L2_xcond_w_qkv, L2_xcond_b_qkv, L2_xcond_w_so, L2_xcond_b_so, L2_xcond_w_q, L2_xcond_b_q, L2_xcond_w_kv, L2_xcond_b_kv, L2_xcond_w_co, L2_xcond_b_co, L2_xcond_w_m1, L2_xcond_b_m1, L2_xcond_w_m2, L2_xcond_b_m2)
    x = _L3_xcond_ref(x, cond_1024[:, None, :], ctx_1024, L3_xcond_ln1_w, L3_xcond_ln1_b, L3_xcond_ln2_w, L3_xcond_ln2_b, L3_xcond_ln3_w, L3_xcond_ln3_b, L3_xcond_qkv_w, L3_xcond_sa_out_w, L3_xcond_q_w, L3_xcond_k_w, L3_xcond_v_w, L3_xcond_ca_out_w, L3_xcond_ffn_w1, L3_xcond_ffn_b1, L3_xcond_ffn_w2, L3_xcond_ffn_b2)
    return x

_drawn_inputs = setup_inputs


def setup_inputs(seed=0):
    import zlib

    import numpy as np

    out = dict(_drawn_inputs(seed))
    spreads = {'L0_xcond_norm1_w': (1.0, 0.6),
     'L0_xcond_normc_w': (1.0, 0.6),
     'L0_xcond_norm2_w': (1.0, 0.6),
     'L1_xcond_b_mod': (0.0, 0.1),
     'L1_xcond_b_qkv': (0.0, 0.1),
     'L1_xcond_b_proj': (0.0, 0.1),
     'L1_xcond_b_qc': (0.0, 0.446),
     'L1_xcond_b_kvc': (0.0, 0.1),
     'L1_xcond_b_cproj': (0.0, 0.1),
     'L1_xcond_b_mlp1': (0.0, 0.1),
     'L1_xcond_b_mlp2': (0.0, 0.1),
     'L2_xcond_b_ada': (0.0, 0.584),
     'L2_xcond_b_qkv': (0.0, 0.8),
     'L2_xcond_b_so': (0.0, 0.461),
     'L2_xcond_b_q': (0.0, 0.8),
     'L2_xcond_b_kv': (0.0, 0.8),
     'L2_xcond_b_co': (0.0, 0.414),
     'L2_xcond_b_m1': (0.0, 0.8),
     'L2_xcond_b_m2': (0.0, 2.0)}
    factors = {'L0_xcond_adaLN_b': 8.0,
     'L0_xcond_qkv_W': 3.243,
     'L0_xcond_attn_out_W': 2.722,
     'L0_xcond_cq_W': 8.0,
     'L0_xcond_ck_W': 8.0,
     'L0_xcond_co_W': 2.777,
     'L0_xcond_mlp_b1': 8.0,
     'L0_xcond_mlp_b2': 8.0,
     'L2_xcond_w_qkv': 4.976,
     'L2_xcond_w_so': 4.635,
     'L2_xcond_w_q': 8.0,
     'L2_xcond_w_kv': 5.279,
     'L2_xcond_w_co': 4.356,
     'L2_xcond_w_m1': 8.0,
     'L2_xcond_w_m2': 8.0,
     'L3_xcond_ln1_b': 64.0,
     'L3_xcond_ln2_w': 64.0,
     'L3_xcond_ln2_b': 64.0,
     'L3_xcond_ln3_b': 64.0,
     'L3_xcond_q_w': 64.0,
     'L3_xcond_k_w': 64.0,
     'L3_xcond_ffn_b1': 64.0,
     'L3_xcond_ffn_b2': 161.161,
     'L3_xcond_ln1_w': 8.0,
     'L3_xcond_ln3_w': 8.0,
     'L3_xcond_qkv_w': 8.0,
     'L3_xcond_sa_out_w': 8.0,
     'L3_xcond_v_w': 8.0,
     'L3_xcond_ca_out_w': 8.0,
     'L3_xcond_ffn_w1': 8.0,
     'L3_xcond_ffn_w2': 8.0}
    for name, (base, spread) in spreads.items():
        noise = np.random.default_rng([zlib.crc32(name.encode()), seed]).standard_normal(out[name].shape)
        drawn = base * np.exp(spread * noise) if base else spread * noise
        out[name] = jnp.asarray(drawn.astype(out[name].dtype))
    for name, factor in factors.items():
        out[name] = (out[name] * factor).astype(out[name].dtype)
    return out
```

```python
from contextlib import ExitStack

import numpy as np
import concourse.bass as bass
from concourse import mybir

BATCH, TOKENS, FEAT = 2, 1024, 256
HEADS, HEAD = 16, 16
CTX = 77
HIDDEN = 1024
TOPK = 16
WINDOW, SHIFT = 128, 64
P = 128
KF = FEAT // P
TILES = TOKENS // P
GROUP = 4
GROUPS = HEADS // GROUP
BLOCK = 512
BLOCKS = TOKENS // BLOCK
PARTS = 6 * HEAD
ROWS = PARTS + 3
PART_OF = {"q": (0, 0, 0, 1, 1, 2), "k": (0, 1, 2, 0, 1, 0)}
VCOLS = 2 * HEAD
A_SLOTS, B_SLOTS, RING = 2, 3, 3
LEAD = 10
NEG = -float(2.0 ** 100)
GONE = -3.0e38

LAYERS = [
    dict(name="L0", eps=1e-5, rope=512, cross_rope=0, mask=True, kind="full", silu_cond=False, act="tanh",
         mod=["adaLN_W"], gates=(2, 5, 8), norms=[(1, 0), (4, 3), (7, 6)]),
    dict(name="L1", eps=1e-6, rope=0, cross_rope=0, mask=False, kind="full", silu_cond=True, act="tanh",
         gates=(2, None, 5), norms=[(1, 0), None, (4, 3)]),
    dict(name="L2", eps=1e-6, rope=0, cross_rope=0, mask=False, kind="window", silu_cond=True, act="swiglu",
         gates=(2, 5, 8), norms=[(1, 0), (4, 3), (7, 6)]),
    dict(name="L3", eps=1e-5, rope=1024, cross_rope=1024, mask=False, kind="full", silu_cond=False, act="erf",
         gates=(None, None, None), norms=[(0, 1), (0, 1), (0, 1)]),
]
NORMS = [(l, i) for l, cfg in enumerate(LAYERS) for i in range(3) if cfg["norms"][i] is not None]
NCOLS = len(NORMS) * 2 * KF


class Step(dict):

    def __getattr__(self, name):
        return self[name]

    def __setattr__(self, name, value):
        self[name] = value


def plan():
    steps = []
    count = dict(m=0, a=1, b=0, c=0, split=0, pv=0, xn=0, xadd=0, group=0, q=0, k=0, od=0, gate=0,
                 ost=0, stats=0, topk=0)
    all_groups = []
    turned_topk = []
    turned = []
    maxima = [0] * RING
    filled = [0] * RING

    def take(kind, n=1):
        count[kind] += n
        return count[kind] - n

    def add(kind, **kw):
        s = Step(kind=kind, **kw)
        steps.append(s)
        return s

    def norm_steps(l, i):
        last = []
        for b in range(BATCH):
            n = take("stats")
            add("stats", l=l, i=i, b=b, stats=n, xadd=count["xadd"])
            for blk in range(BLOCKS):
                s = add("norm", l=l, i=i, b=b, blk=blk, b0=take("b", KF), xn=take("xn"), stats=n)
                turned.append(s.b0 + KF)
                s.xn_b = turned[-3] if len(turned) > 2 else 0
            last.append(s.b0 + KF - 1)
        return last

    def project(l, which, b, hh, blk, ht, rope, whiches_cross):
        s = add("project", l=l, which=which, b=b, hh=hh, blk=blk, ht=ht, bn=take("b"), rope=rope,
                split=take("split"), width=BLOCK, cross=whiches_cross)
        return s

    def rotate(s):
        if s.rope:
            s.an = take("a")
            add("rotate", of=s)
        s.written = count[s.which]
        add("split", of=s)
        if s.blk == BLOCKS - 1:
            buf = s.which
            take(buf)
            add("scratch", of=s)

    def projections(l, b, whiches, ht, rope):
        late = None
        for hh in range(KF):
            for which in whiches:
                for blk in range(BLOCKS):
                    s = project(l, which, b, hh, blk, ht[b], rope, len(whiches) == 1)
                    if late is not None:
                        rotate(late)
                        yield
                    late = s
        rotate(late)
        yield

    def attention(l, cross, ht):
        cfg = LAYERS[l]
        kind = "topk" if cross and cfg["kind"] == "window" else "cross" if cross else cfg["kind"]
        whiches = ("q",) if cross else ("q", "k")
        first, second = [], []
        groups = []
        for n in range(BATCH * GROUPS):
            g = Step(l=l, cross=cross, akind=kind, b=n // GROUPS, g=n % GROUPS, local=n, n=take("group"))
            g.m = take("m") if kind != "topk" else None
            g.slot = g.n % RING
            groups.append(g)
            all_groups.append(g)
        for g in groups:
            if g.g == 0:
                first.append(("project", g.b))
            first.append(("load", g))
            units = {"full": GROUP * TILES, "window": GROUP, "cross": TILES // 2, "topk": TILES // 2}[kind]
            if kind != "topk":
                first += [("first", g, u) for u in range(units)]
                first.append(("max", g))
        for g in groups:
            if g.g == 0 and not cross:
                second.append(("v", g))
            keys = TILES if kind == "full" else 1
            for qh in range(BLOCKS):
                for kt in range(keys):
                    second.append(("second", g, qh, kt, kt == keys - 1))
            second.append(("end", g))
        pos = 0
        emitted = {}

        def do_first():
            nonlocal pos
            item = first[pos]
            pos += 1
            if item[0] == "project":
                for _ in projections(l, item[1], whiches, ht, cfg["cross_rope" if cross else "rope"]):
                    pass
                return 0
            if item[0] == "load":
                g = item[1]
                g.written = {w: count[w] for w in whiches}
                g.before = all_groups[g.n - RING] if g.n >= RING else None
                filled[g.slot] += len(whiches)
                g.filled = filled[g.slot]
                add("load", g=g)
                return 0
            if item[0] == "first":
                _, g, u = item
                add("first", g=g, u=u, an=take("a"))
                g.last_a = count["a"] - 1
                return 1
            g = item[1]
            g.max_b = take("b")
            maxima[g.slot] += 1
            g.max_filled = maxima[g.slot]
            add("max", g=g, m=g.m)
            emitted[g.n] = True
            return 0

        def run_first(units, until=None):
            nonlocal pos
            done = 0
            while pos < len(first):
                if until is not None:
                    if until in emitted:
                        return
                elif done >= units:
                    if first[pos][0] != "max":
                        return
                done += do_first()

        per_group = {"full": GROUP * TILES, "window": GROUP, "cross": TILES // 2, "topk": 0}[kind]
        total_steps = BLOCKS * (TILES if kind == "full" else 1)
        per_step = per_group // total_steps if per_group else 0
        lead = LEAD if kind == "full" else per_group // 2
        if kind == "topk":
            run_first(0)
            while pos < len(first) and not (first[pos][0] == "load" and first[pos][1].local >= 2):
                do_first()
        else:
            run_first(0, until=groups[0].n)
            run_first(lead)
        vlast = count["a"] - 1
        pending = None
        late = []

        def tick():
            for item in list(late):
                item[0] -= 1
                if item[0] <= 0:
                    late.remove(item)
                    item[1]()

        def emit_pv():
            nonlocal pending
            if pending is None:
                return
            s = pending
            pending = None
            take("pv")
            if s.kt == 0:
                s.g.cn = take("c")
            s.cn = s.g.cn
            add("pv", of=s)
            if s.last:
                s.ost = take("ost")
                add("out_stage", of=s)

        def out_of(g):
            s = add("dense", l=l, b=g.b, hh=g.g // 2, n=take("od"), ost=g.ost_last, akind=kind)
            late.append([3 if kind == "full" else 1, lambda: add("normalise", of=s)])
            if g.g == GROUPS - 1:
                def out():
                    for u in range(TILES // 2):
                        add("out", l=l, cross=cross, b=g.b, u=u, an=take("a"), od=count["od"], xadd=take("xadd"),
                            gate=gates_seen)
                late.append([6 if kind == "full" else 2, out])

        for item in second:
            if item[0] == "v":
                g = item[1]
                emit_pv()
                for u in range(2):
                    add("v", l=l, b=g.b, u=u, an=take("a"), pv=count["pv"], ht=ht[g.b])
                    g.v_a = count["a"] - 1
                vlast = count["a"] - 1
            elif item[0] == "second":
                _, g, qh, kt, last = item
                if kind == "topk":
                    while pos < len(first) and first[pos][0] != "project" and (
                            first[pos][1].local <= g.local + 1):
                        do_first()
                    if g.g == GROUPS - 1 and qh == 0:
                        while pos < len(first) and (first[pos][0] == "project" or first[pos][1].local <= g.local + 1):
                            do_first()
                elif g.n not in emitted:
                    run_first(0, until=g.n)
                s = Step(g=g, qh=qh, kt=kt, last=last, v_a=vlast)
                if kind == "topk":
                    for t in range(TILES // BLOCKS // 2):
                        k = add("topk", of=s, g=g, qh=qh, t=t, an=take("a"), n=take("topk"))
                        s.topk = k
                        emit_pv()
                        k.bn = take("b", 2)
                        k.ep_b = turned_topk[-1] if turned_topk else 0
                        turned_topk.append(k.bn + 2)
                        add("topk_turn", of=k)
                    s.last_b = count["b"] - 1
                else:
                    add("scores", of=s, h0=0, bn=take("b", 2))
                    run_first(per_step // 2)
                    add("scores", of=s, h0=2, bn=take("b", 2))
                    s.last_b = count["b"] - 1
                    run_first(per_step - per_step // 2)
                    emit_pv()
                pending = s
                s.pv = count["pv"]
                tick()
            else:
                g = item[1]
                emit_pv()
                g.ost_last = count["ost"] - 1
                g.pv_last = count["pv"] - 1
                if g.g % 2 == 1:
                    out_of(g)
        while late:
            tick()

    gates_seen = 0
    for l, cfg in enumerate(LAYERS):
        ht = norm_steps(l, 0)
        gates_seen += int(cfg["gates"][0] is not None)
        add("gate", l=l, i=0, an=take("a") if cfg["gates"][0] is not None else None, xadd=count["xadd"])
        attention(l, False, ht)
        ht = norm_steps(l, 1)
        gates_seen += int(cfg["gates"][1] is not None)
        add("gate", l=l, i=1, an=take("a") if cfg["gates"][1] is not None else None, xadd=count["xadd"])
        if l == 1:
            c = add("context_norm", l=l, b0=take("b", KF), stats=take("stats"), xn=take("xn"))
            turned.append(c.b0 + KF)
        else:
            add("context_norm", l=l, b0=None)
        for hh in range(KF):
            s = add("project", l=l, which="ck", b=0, hh=hh, blk=0, ht=None, bn=take("b"), rope=cfg["cross_rope"],
                    split=take("split"), width=BATCH * CTX, cross=True)
            if s.rope:
                s.an = take("a")
                add("rotate", of=s)
            s.written = count["k"]
            add("split", of=s)
            take("k")
            add("ctx_scratch", of=s)
        add("ctx_load", l=l, written=count["k"], pv=count["pv"])
        for b in range(BATCH):
            add("ctx_v", l=l, b=b, an=take("a"))
        attention(l, True, ht)
        ht = norm_steps(l, 2)
        gates_seen += int(cfg["gates"][2] is not None)
        add("gate", l=l, i=2, an=take("a") if cfg["gates"][2] is not None else None, xadd=count["xadd"])
        pend = None

        def down(h):
            for u in range(BLOCK // P // 2):
                add("down", l=l, b=h.b, blk=h.blk, u=u, an=take("a"), xadd=take("xadd"), par=h.par,
                    hid_b=h.hid_b, hid_a=h.hid_a, gate=gates_seen)
            if l == len(LAYERS) - 1:
                add("store", b=h.b, blk=h.blk, xadd=count["xadd"])
        for blk in range(BATCH * BLOCKS):
            h = Step(b=blk // BLOCKS, blk=blk % BLOCKS, par=blk % 2, n=blk)
            for j in range(HIDDEN // P):
                s = add("up", l=l, b=h.b, blk=h.blk, j=j, bn=take("b"), par=h.par, n=h.n, ht=ht[h.b],
                        an=take("a") if cfg["act"] == "swiglu" else None)
            h.hid_b, h.hid_a = count["b"], count["a"]
            if pend is not None:
                down(pend)
            pend = h
        down(pend)
    return steps, count


def blocks_kernel(nc, ins, out):
    f32, bf16, u8 = mybir.dt.float32, mybir.dt.bfloat16, mybir.dt.uint8
    ALU, ACT, AX = mybir.AluOpType, mybir.ActivationFunctionType, mybir.AxisListType
    steps, total = plan()
    ctx = ExitStack()
    with ctx:
        def sb(name, shape, dt=f32):
            return ctx.enter_context(nc.sbuf_tensor(name, shape, dt))

        def sem(name):
            return ctx.enter_context(nc.semaphore(name))

        X = sb("x_tok", [P, BATCH * TILES, FEAT])
        HT = sb("h_feat", [P, KF, BATCH, TOKENS])
        RINGS = sb("rings", [P, 2, RING * GROUP * TOKENS // 2])
        Q6 = RINGS[:, 0, :].bitcast(bf16).rearrange("p (s h t) -> p s h t", s=RING, h=GROUP)
        K6 = RINGS[:, 1, :].bitcast(bf16).rearrange("p (s h t) -> p s h t", s=RING, h=GROUP)
        KC = RINGS[:, 1, :].bitcast(bf16).rearrange("p (s t) -> p s t", s=RING)[:, :, 0:HEADS * 80]\
            .rearrange("p s (h t) -> p s h t", t=80)
        WORK = sb("work", [P, 5120])
        RAW = WORK[:, 0:1024].rearrange("p (s t) -> p s t", s=2)
        ROT = WORK[:, 1024:1536]
        CTN = WORK[:, 1536:1536 + KF * BATCH * CTX].rearrange("p (k t) -> p k t", k=KF)
        SPLIT = {w: WORK[:, o:o + 1536].bitcast(bf16).rearrange("p (j t) -> p j t", j=3)
                 for w, o in (("q", 2048), ("k", 3584))}
        HID = [RINGS[:, 0, 0:4096].rearrange("p (j t) -> p j t", j=HIDDEN // P),
               WORK[:, 0:4096].rearrange("p (j t) -> p j t", j=HIDDEN // P)]
        VA = sb("v_and_ones", [P, TILES, HEADS, VCOLS])
        PT = sb("probs", [P, 2, GROUP, BLOCK])
        XN = PT[:, 0, :, :].rearrange("p (s c) t -> p s (c t)", s=2).rearrange("p s (c t) -> p s c t", t=FEAT)
        OST = sb("out_stage", [P, 2, BLOCK])
        DEN = sb("denominators", [P, TOKENS])
        GW = DEN[:, 0:KF * FEAT].rearrange("p (k f) -> p k f", k=KF)
        WR = sb("w_mlp", [P, 8192])
        MASKT = WR[:, 0:4096].bitcast(bf16).rearrange("p (t q) -> p t q", t=TILES)
        MASKQ = WR[:, 4096:8192].bitcast(bf16).rearrange("p (t q) -> p t q", t=TILES)
        W2 = WR[:, 4096:6144].rearrange("p (k f) -> p k f", k=HIDDEN // P)
        ROPE_L3 = WR[:, 6144:8192].rearrange("p (c t) -> p c t", c=2)
        NSC = 2 * GROUP * CTX
        TS = WR[:, 6144:6144 + 2 * NSC].rearrange("p (s i k) -> p s i k", s=2, k=CTX)
        EP = WR[:, 6144 + 2 * NSC:6144 + 3 * NSC].rearrange("p (i k) -> p i k", k=CTX)
        S3 = RINGS[:, 1, 4096:4096 + 2 * NSC].rearrange("p (s i k) -> p s i k", s=2, k=CTX)
        WQKV = sb("w_qkv", [P, KF, 3 * FEAT])
        WO = sb("w_out", [P, KF, FEAT])
        WCQ = sb("w_cross_q", [P, KF, FEAT])
        WCKV = sb("w_cross_kv", [P, KF, 2 * FEAT])
        MISC = sb("rope0_or_context", [P, 1024])
        ROPE_L0 = MISC[:, :].rearrange("p (c t) -> p c t", c=2)
        CTOK = MISC[0:CTX, 0:512].rearrange("p (b f) -> p b f", b=BATCH)
        CNRM = MISC[0:CTX, 512:1024].rearrange("p (b f) -> p b f", b=BATCH)
        GB = sb("gates", [P, BATCH, 2, FEAT])
        TMP = sb("branch_out", [P, 2, FEAT])
        BB = sb("row_biases", [P, 3, FEAT])
        CTXT = sb("ctx_feat", [P, KF, BATCH * CTX])
        IDF = sb("ident_f", [P, P])
        IDB = sb("ident_b", [P, P], bf16)
        ROTM = sb("rot_matrix", [P, P])
        COND = sb("cond", [P, 2, KF, BATCH])
        MODC = sb("mod_cols", [P, NCOLS, BATCH])
        MODB = sb("mod_bias_and_weight", [P, 2, NCOLS])
        COLS = sb("bias_cols", [P, 4, 24])
        STAT = sb("bn_stats", [P, TILES, 6])
        MV = sb("mean_var", [P, BATCH, TILES, 2])
        RSTD = sb("rstd", [P, BATCH, TILES])
        NM = sb("row_max", [P, 2, GROUP * TILES])
        NT = sb("neg_max", [GROUP * TILES, 2, P])
        MS = sb("neg_max_parts", [GROUP * TILES, 2, 3, P], bf16)
        JUNK = sb("masked_scores", [P, TOKENS], bf16)
        M8 = WORK[:, 1848:1976].rearrange("p (s i k) -> p s i k", s=2, k=8)
        M8B = WORK[:, 1976:2040].rearrange("p (i k) -> p i k", k=8)
        MROW = WORK[0:1, 1848:1848 + CTX].bitcast(bf16).rearrange("p (b t) -> p b t", b=BATCH)
        MCOL = sb("kv_mask_col", [CTX, BATCH])
        ONE = WORK[0:1, 1928:1928 + P // 2].bitcast(bf16)

        PA = ctx.enter_context(nc.psum_tensor("ring_a", [P, A_SLOTS, 1024], f32))
        PB = ctx.enter_context(nc.psum_tensor("ring_b", [P, B_SLOTS, BLOCK], f32))
        PC = ctx.enter_context(nc.psum_tensor("ring_c", [P, BLOCK], f32))

        QK_SCR = {w: nc.dram_tensor(f"scr_{w}", [BATCH, HEADS, 6, HEAD, TOKENS], bf16, kind="Internal").ap()
                  for w in "qk"}
        KC_SCR = nc.dram_tensor("scr_ctx_k", [HEADS, 6, HEAD, BATCH * CTX], bf16, kind="Internal").ap()
        MX_SCR = nc.dram_tensor("scr_max", [2, 3, GROUP * TILES, P], bf16, kind="Internal").ap()
        O_SCR = nc.dram_tensor("scr_out", [BATCH, HEADS, VCOLS, TOKENS], f32, kind="Internal").ap()

        a_full, a_evac = sem("ring_a_filled"), sem("ring_a_evacuated")
        b_full, b_evac = sem("ring_b_filled"), sem("ring_b_evacuated")
        c_evac = sem("ring_c_evacuated")
        pv_done = sem("products_with_v")
        consts_in, x_in, modw_in, mask_in = sem("consts_in"), sem("x_in"), sem("mod_weights_in"), sem("masks_in")
        cond_ready, mod_ready, setup_dve = sem("cond_silu"), sem("mod_cols_ready"), sem("dve_setup_done")
        k_ones, mask_ready = sem("k_ones_ready"), sem("mask_bias_ready")
        w_in = {n: sem("in_" + n) for n in ("qkv", "o", "cq", "ckv", "w1", "w2", "gate", "rows", "misc", "rope3")}
        stats_ready, rstd_ready, xn_ready, xn_used = sem("stats_ready"), sem("roots_ready"), sem("xn_ready"), sem("xn_used")
        split_done = sem("split_done")
        rot_ready = sem("rotated_read")
        scr_in = {w: sem("scratch_written_" + w) for w in "qk"}
        kc_in = sem("context_keys_in")
        ring_in = [sem(f"ring_loaded_{i}") for i in range(RING)]
        max_split, mx_out = sem("max_parts_ready"), sem("max_parts_out")
        max_in = [sem(f"max_rows_in_{i}") for i in range(RING)]
        ost_out = [sem(f"out_stage_written_{i}") for i in range(2)]
        od_in, norm_done, x_add = sem("dense_out_in"), sem("out_normalised"), sem("residual_added")
        tk_sel, tk_arg, tk_exp = sem("top_k_marked"), sem("top_k_arguments"), sem("top_k_exps")
        gate_ready = sem("gate_ready")
        dve_step, pool_step, act_step = sem("dve_step"), sem("pool_step"), sem("act_step")
        stored = sem("stored")

        def bcast(ap, n):
            return ap.unsqueeze(1).broadcast_to([ap.shape[0], n, ap.shape[-1]])

        def w1_view(l):
            n = 2 * HIDDEN if LAYERS[l]["act"] == "swiglu" else HIDDEN
            return WR[:, 0:KF * n].rearrange("p (k f) -> p k f", k=KF)

        def mod_col(l, i, s, kf):
            return (NORMS.index((l, i)) * 2 + s) * KF + kf

        rope_of = {0: ROPE_L0, 3: ROPE_L3}

        def rope_cols(s, c):
            t = rope_of[s.l][:, c, :]
            if s.which == "ck":
                return bcast(t[:, 0:CTX], BATCH)
            at = (s.blk * BLOCK) % s.rope
            return t[:, at:at + BLOCK]

        def tok_view(ap, s):
            return ap[:, 0:s.width].rearrange("p (b t) -> p b t", b=BATCH) if s.which == "ck" else ap[:, 0:s.width]

        def keys_of(g):
            return CTX if g.cross else P

        block = ctx.enter_context(nc.Block())

        @block.sync
        def _(sp):
            def weight(name, dst, src):
                sp.dma_start(dst, src).then_inc(w_in[name], 16)

            def kp(w):
                return w.rearrange("(k p) f -> p k f", p=P)

            def row(v):
                return v.rearrange("(o f) -> o f", o=1).broadcast_to([P, v.shape[0]])

            for dst, src in ((IDF[:], ins["ident"]), (ROTM[:], ins["rotm"]),
                             (COND[:, 0], ins["cond"]), (MODB[:], ins["modb"]), (COLS[:], ins["cols"]),
                             (CTXT[:], ins["ctxt"]), (MISC[:], ins["rope0"])):
                sp.dma_start(dst, src).then_inc(consts_in, 16)
            for b in range(BATCH):
                sp.dma_start(X[:, b * TILES:(b + 1) * TILES, :],
                             ins["x"][b].rearrange("(t p) f -> p t f", p=P)).then_inc(x_in, 16)
            MODW = RINGS[:, :, :].rearrange("p a t -> p (a t)")[:, 0:KF * NCOLS // KF * FEAT]\
                .rearrange("p (k e f) -> p k e f", k=KF, e=NCOLS // KF)
            for e, (l, i) in enumerate(NORMS):
                for s in range(2):
                    src = ins[f"mod_{l}_{i}"][:, s * FEAT:(s + 1) * FEAT] if l == 3 else \
                        ins[f"mod_{l}"][:, LAYERS[l]["norms"][i][s] * FEAT:(LAYERS[l]["norms"][i][s] + 1) * FEAT]
                    sp.dma_start(MODW[:, :, e * 2 + s, :], kp(src)).then_inc(modw_in, 16)
            raw = PT[:, :, :, :].rearrange("p s h t -> p (s h t)")
            sp.dma_start(raw[:, 0:2048].bitcast(u8).rearrange("p (t q) -> p t q", t=TILES),
                         ins["mask_t"].rearrange("(t p) q -> p t q", p=P)).then_inc(mask_in, 16)
            sp.dma_start(raw[:, 2048:4096].bitcast(u8).rearrange("p (t q) -> p t q", t=TILES),
                         ins["mask_q"].rearrange("(t p) q -> p t q", p=P)).then_inc(mask_in, 16)
            sp.dma_start(JUNK[0:1, 0:BATCH * CTX // 2].bitcast(u8), ins["kv_row"]).then_inc(mask_in, 16)
            sp.dma_start(JUNK[0:CTX, 512:512 + BATCH // 2].bitcast(u8), ins["kv_col"]).then_inc(mask_in, 16)
            weight("qkv", WQKV[:], kp(ins["qkv_0"]))
            weight("o", WO[:], kp(ins["o_0"]))
            weight("cq", WCQ[:], kp(ins["cq_0"]))
            weight("ckv", WCKV[:], kp(ins["ckv_0"]))

            od = 0
            for s in steps:
                if s.kind == "gate":
                    if s.xadd:
                        sp.wait_ge(x_add, s.xadd)
                    l, i = s.l, s.i
                    if s.an is not None:
                        c = LAYERS[l]["gates"][i]
                        weight("gate", GW, kp(ins[f"mod_{l}"][:, c * FEAT:(c + 1) * FEAT]))
                    for j, name in enumerate((f"gb_{l}_{i}", f"ob_{l}_{i}", f"vb_{l}_{i}")):
                        weight("rows", BB[:, j, :], row(ins[name]))
                    if i == 1:
                        weight("o", WO[:], kp(ins[f"co_{l}"]))
                        weight("w1", w1_view(l), kp(ins[f"w1_{l}"]))
                        weight("w2", W2, kp(ins[f"w2_{l}"]))
                        if l + 1 < len(LAYERS):
                            weight("qkv", WQKV[:], kp(ins[f"qkv_{l + 1}"]))
                    if i == 2 and l + 1 < len(LAYERS):
                        weight("o", WO[:], kp(ins[f"o_{l + 1}"]))
                        weight("cq", WCQ[:], kp(ins[f"cq_{l + 1}"]))
                        weight("ckv", WCKV[:], kp(ins[f"ckv_{l + 1}"]))
                        if l == 0:
                            weight("misc", CTOK, ins["ctx"].rearrange("b t f -> t b f"))
                        if l == 2:
                            weight("rope3", WR[:, 6144:8192], ins["rope3"])
                elif s.kind == "scratch":
                    s = s.of
                    sp.wait_ge(split_done, s.split + 1)
                    for j, part in enumerate(PART_OF[s.which]):
                        sp.dma_start(QK_SCR[s.which][s.b, s.hh * 8:s.hh * 8 + 8, j], SPLIT[s.which][:, part, :])\
                            .then_inc(scr_in[s.which], 16)
                elif s.kind == "ctx_scratch":
                    s = s.of
                    sp.wait_ge(split_done, s.split + 1)
                    for j, part in enumerate(PART_OF["k"]):
                        sp.dma_start(KC_SCR[s.hh * 8:s.hh * 8 + 8, j], SPLIT["k"][:, part, 0:BATCH * CTX])\
                            .then_inc(scr_in["k"], 16)
                elif s.kind == "ctx_load":
                    sp.wait_ge(scr_in["k"], 96 * s.written)
                    sp.wait_ge(pv_done, s.pv)
                    for b in range(BATCH):
                        sp.dma_start(KC[0:PARTS, b, :, 0:CTX],
                                     KC_SCR[:, :, :, b * CTX:(b + 1) * CTX].rearrange("h j d t -> (j d) h t"))\
                            .then_inc(kc_in, 16)
                elif s.kind == "load":
                    g = s.g
                    if g.before is not None:
                        sp.wait_ge(pv_done, g.before.pv_last + 1)
                    for w, ring in (("q", Q6), ("k", K6)):
                        if w in g.written:
                            sp.wait_ge(scr_in[w], 96 * g.written[w])
                            sp.dma_start(ring[0:PARTS, g.slot], QK_SCR[w][g.b, g.g * GROUP:(g.g + 1) * GROUP]
                                         .rearrange("h j d t -> (j d) h t")).then_inc(ring_in[g.slot], 16)
                elif s.kind == "max":
                    n = s.m
                    sp.wait_ge(max_split, n + 1)
                    sp.dma_start(MX_SCR[n % 2].rearrange("j r t -> r j t"), MS[:, n % 2]).then_inc(mx_out, 16)
                    sp.wait_ge(mx_out, 16 * (n + 1))
                    sp.dma_start(Q6[PARTS:ROWS, s.g.slot].rearrange("p h t -> p (h t)"),
                                 MX_SCR[n % 2].rearrange("j r t -> j (r t)")).then_inc(max_in[s.g.slot], 16)
                elif s.kind == "out_stage":
                    s = s.of
                    sp.wait_ge(c_evac, s.cn + 1)
                    sp.dma_start(O_SCR[s.g.b, s.g.g * GROUP:(s.g.g + 1) * GROUP, :, s.qh * BLOCK:(s.qh + 1) * BLOCK],
                                 OST[:, s.ost % 2, :]).then_inc(ost_out[s.ost % 2], 16)
                elif s.kind == "dense":
                    sp.wait_ge(ost_out[0], 16 * ((s.ost + 2) // 2))
                    if s.ost >= 1:
                        sp.wait_ge(ost_out[1], 16 * ((s.ost + 1) // 2))
                    if s.n:
                        sp.wait_ge(norm_done, s.n)
                    cuts = [(0, TOKENS, 0)]
                    if s.akind == "window":
                        cuts = [(SHIFT, TOKENS, 0), (0, SHIFT, TOKENS - SHIFT)]
                    for lo, hi, at in cuts:
                        for dst, r0 in ((HT[:, s.hh, s.b, lo:hi], 0), (DEN[:, lo:hi], HEAD)):
                            sp.dma_start(dst, O_SCR[s.b, s.hh * 8:s.hh * 8 + 8, r0:r0 + HEAD, at:at + hi - lo])\
                                .then_inc(od_in, 16)
                            od += 16
                    s.need = od
                elif s.kind == "store":
                    sp.wait_ge(x_add, s.xadd)
                    t = BLOCK // P
                    sp.dma_start(out[s.b, s.blk * BLOCK:(s.blk + 1) * BLOCK].rearrange("(t p) f -> p t f", p=P),
                                 X[:, s.b * TILES + s.blk * t:s.b * TILES + (s.blk + 1) * t, :]).then_inc(stored, 16)
            sp.wait_ge(stored, 16 * BATCH * BLOCKS)

        @block.tensor
        def _(pe):
            def need_a(n):
                if n >= A_SLOTS:
                    pe.wait_ge(a_evac, n - A_SLOTS + 1)
                return PA[:, n % A_SLOTS, :]

            def need_b(n):
                if n >= B_SLOTS:
                    pe.wait_ge(b_evac, n - B_SLOTS + 1)
                return PB[:, n % B_SLOTS, :]

            mm = nc.tensor.matmul
            MODW = RINGS[:, :, :].rearrange("p a t -> p (a t)")[:, 0:KF * NCOLS // KF * FEAT]\
                .rearrange("p (k e f) -> p k e f", k=KF, e=NCOLS // KF)
            pe.wait_ge(cond_ready, 1)
            pe.wait_ge(modw_in, 16 * 2 * len(NORMS))
            ps = PA[:, 0, :].rearrange("p (c b) -> p c b", b=BATCH)
            for e, (l, i) in enumerate(NORMS):
                for s in range(2):
                    for m in range(KF):
                        c = (e * 2 + s) * KF + m
                        for k in range(KF):
                            last = mm(ps[:, c, :], MODW[:, k, e * 2 + s, m * P:(m + 1) * P],
                                      COND[:, int(LAYERS[l]["silu_cond"]), k, :], start=k == 0, stop=k == KF - 1)
            last.then_inc(a_full, 1)
            n_o = n_gate = 0
            for s in steps:
                if s.kind == "norm":
                    pe.wait_ge(xn_ready, s.xn + 1)
                    for kf in range(KF):
                        ps = need_b(s.b0 + kf)
                        for t in range(BLOCK // P):
                            last = nc.tensor.transpose(ps[:, t * P:(t + 1) * P],
                                                       XN[:, s.xn % 2, t, kf * P:(kf + 1) * P], IDF[:])
                        last.then_inc(b_full, 1)
                elif s.kind == "gate" and s.an is not None:
                    n_gate += 1
                    pe.wait_ge(w_in["gate"], 16 * n_gate)
                    ps = need_a(s.an)
                    for b in range(BATCH):
                        for k in range(KF):
                            c = COND[:, int(LAYERS[s.l]["silu_cond"]), k, b:b + 1].broadcast_to([P, P])
                            last = mm(ps[:, b * FEAT:(b + 1) * FEAT], c, GW[:, k, :], start=k == 0, stop=k == KF - 1)
                    last.then_inc(a_full, 1)
                elif s.kind == "context_norm" and s.b0 is not None:
                    pe.wait_ge(xn_ready, s.xn + 1)
                    for kf in range(KF):
                        ps = need_b(s.b0 + kf)
                        for b in range(BATCH):
                            last = nc.tensor.transpose(ps[:, b * CTX:(b + 1) * CTX],
                                                       CNRM[:, b, kf * P:(kf + 1) * P], IDF[0:CTX, 0:CTX])
                        last.then_inc(b_full, 1)
                elif s.kind == "project":
                    if s.which == "ck":
                        pe.wait_ge(w_in["ckv"], 16 * (s.l + 1))
                        w, at = WCKV, 0
                        src = CTN if s.l == 1 else CTXT
                        if s.l == 1:
                            pe.wait_ge(b_evac, s.bn - s.hh)
                    else:
                        pe.wait_ge(b_evac, s.ht + 1)
                        if s.cross:
                            pe.wait_ge(w_in["cq"], 16 * (s.l + 1))
                            w, at = WCQ, 0
                        else:
                            pe.wait_ge(w_in["qkv"], 16 * (s.l + 1))
                            w, at = WQKV, FEAT * (s.which == "k")
                        src = HT[:, :, s.b, s.blk * BLOCK:(s.blk + 1) * BLOCK]
                    ps = need_b(s.bn)
                    for k in range(KF):
                        last = mm(ps[:, 0:s.width], w[:, k, at + s.hh * P:at + (s.hh + 1) * P], src[:, k, 0:s.width],
                                  start=k == 0, stop=k == KF - 1)
                    last.then_inc(b_full, 1)
                elif s.kind == "rotate":
                    s = s.of
                    pe.wait_ge(b_evac, s.bn + 1)
                    mm(need_a(s.an)[:, 0:s.width], ROTM[:], RAW[:, s.split % 2, 0:s.width],
                       start=True, stop=True).then_inc(a_full, 1)
                elif s.kind == "v":
                    pe.wait_ge(b_evac, s.ht + 1)
                    ps = need_a(s.an)
                    for t in range(4):
                        tok = (s.u * 4 + t) * P
                        for k in range(KF):
                            last = mm(ps[:, t * FEAT:(t + 1) * FEAT], HT[:, k, s.b, tok:tok + P],
                                      WQKV[:, k, 2 * FEAT:3 * FEAT], start=k == 0, stop=k == KF - 1)
                    last.then_inc(a_full, 1)
                elif s.kind == "ctx_v":
                    ps = need_a(s.an)
                    src = CTN if s.l == 1 else CTXT
                    for k in range(KF):
                        last = mm(ps[0:CTX, 0:FEAT], src[:, k, s.b * CTX:(s.b + 1) * CTX],
                                  WCKV[:, k, FEAT:2 * FEAT], start=k == 0, stop=k == KF - 1)
                    last.then_inc(a_full, 1)
                elif s.kind in ("first", "topk"):
                    g = s.g
                    pe.wait_ge(ring_in[g.slot], 16 * g.filled)
                    if g.cross:
                        pe.wait_ge(kc_in, 32 * (g.l + 1))
                    ps = need_a(s.an)
                    if g.akind == "full":
                        h, t = s.u // TILES, s.u % TILES
                        for half in range(2):
                            last = mm(ps[:, half * BLOCK:(half + 1) * BLOCK], Q6[0:PARTS, g.slot, h, t * P:(t + 1) * P],
                                      K6[0:PARTS, g.slot, h, half * BLOCK:(half + 1) * BLOCK], start=True, stop=True)
                    elif g.akind == "window":
                        for w in range(TILES):
                            last = mm(ps[:, w * P:(w + 1) * P], Q6[0:PARTS, g.slot, s.u, w * P:(w + 1) * P],
                                      K6[0:PARTS, g.slot, s.u, w * P:(w + 1) * P], start=True, stop=True)
                    else:
                        pair = s.u if s.kind == "first" else s.qh * 2 + s.t
                        if g.l == 0:
                            pe.wait_ge(mask_ready, 4)
                        for t in range(2):
                            for h in range(GROUP):
                                at = t * BLOCK + h * P
                                tok = (pair * 2 + t) * P
                                masked = LAYERS[g.l]["mask"]
                                if masked:
                                    mm(ps[:, at:at + CTX], ONE[0:1, :], MROW[0:1, g.b, :], start=True, stop=False)
                                last = mm(ps[:, at:at + CTX], Q6[0:PARTS, g.slot, h, tok:tok + P],
                                          KC[0:PARTS, g.b, g.g * GROUP + h, 0:CTX], start=not masked, stop=True)
                    last.then_inc(a_full, 1)
                elif s.kind == "max":
                    pe.wait_ge(a_evac, s.g.last_a + 1)
                    nc.tensor.transpose(need_b(s.g.max_b)[0:GROUP * TILES, 0:P], NM[:, s.m % 2, :], IDF[:])\
                        .then_inc(b_full, 1)
                elif s.kind == "scores":
                    s, h0, bn = s.of, s.h0, s.bn
                    g = s.g
                    pe.wait_ge(max_in[g.slot], 16 * g.max_filled)
                    pe.wait_ge(k_ones, 2 if g.l == 3 else 1)
                    if g.akind == "full" and LAYERS[g.l]["mask"]:
                        pe.wait_ge(mask_ready, 4)
                    q0 = s.qh * BLOCK
                    for h in (h0, h0 + 1):
                        ps = need_b(bn + h - h0)
                        if g.akind == "full":
                            masked = LAYERS[g.l]["mask"]
                            if masked:
                                mm(ps[:, :], IDB[:], MASKT[:, s.kt, q0:q0 + BLOCK], start=True, stop=False)
                            last = mm(ps[:, :], K6[0:ROWS, g.slot, h, s.kt * P:(s.kt + 1) * P],
                                      Q6[0:ROWS, g.slot, h, q0:q0 + BLOCK], start=not masked, stop=True)
                        elif g.akind == "window":
                            for i in range(BLOCK // WINDOW):
                                w = q0 + i * P
                                last = mm(ps[:, i * P:(i + 1) * P], K6[0:ROWS, g.slot, h, w:w + P],
                                          Q6[0:ROWS, g.slot, h, w:w + P], start=True, stop=True)
                        else:
                            last = mm(ps[0:CTX, :], KC[0:ROWS, g.b, g.g * GROUP + h, 0:CTX],
                                      Q6[0:ROWS, g.slot, h, q0:q0 + BLOCK], start=True, stop=True)
                        last.then_inc(b_full, 1)
                elif s.kind == "topk_turn":
                    k = s.of
                    pe.wait_ge(tk_exp, k.n + 1)
                    for t in range(2):
                        ps = need_b(k.bn + t)
                        for h in range(GROUP):
                            last = nc.tensor.transpose(ps[0:CTX, h * P:(h + 1) * P], EP[:, t * GROUP + h, :], IDF[:])
                        last.then_inc(b_full, 1)
                elif s.kind == "pv":
                    s = s.of
                    g, n = s.g, keys_of(s.g)
                    pe.wait_ge(b_evac, s.last_b + 1)
                    pe.wait_ge(a_evac, s.v_a + 1)
                    if s.kt == 0 and s.cn:
                        pe.wait_ge(c_evac, s.cn)
                    for h in range(GROUP):
                        o = PC[VCOLS * h:VCOLS * (h + 1), :]
                        head = g.g * GROUP + h
                        if g.akind == "window":
                            for i in range(BLOCK // WINDOW):
                                last = mm(o[:, i * P:(i + 1) * P], VA[:, s.qh * 4 + i, head, :],
                                          PT[:, s.pv % 2, h, i * P:(i + 1) * P], start=True, stop=True)
                        else:
                            last = mm(o, VA[0:n, g.b if g.cross else s.kt, head, :], PT[0:n, s.pv % 2, h, :],
                                      start=s.kt == 0, stop=s.last)
                    last.then_inc(pv_done, 1)
                elif s.kind == "out":
                    pe.wait_ge(norm_done, s.od)
                    pe.wait_ge(w_in["o"], 16 * (2 * s.l + int(s.cross) + 1))
                    ps = need_a(s.an)
                    for t in range(2):
                        tok = (s.u * 2 + t) * P
                        for k in range(KF):
                            last = mm(ps[:, t * FEAT:(t + 1) * FEAT], HT[:, k, s.b, tok:tok + P], WO[:, k, :],
                                      start=k == 0, stop=k == KF - 1)
                    last.then_inc(a_full, 1)
                elif s.kind == "up":
                    pe.wait_ge(b_evac, s.ht + 1)
                    pe.wait_ge(w_in["w1"], 16 * (s.l + 1))
                    w1 = w1_view(s.l)
                    for ps, at, full in ((need_b(s.bn), 0, b_full),) + (
                            ((need_a(s.an), HIDDEN, a_full),) if s.an is not None else ()):
                        for k in range(KF):
                            last = mm(ps[:, 0:BLOCK], w1[:, k, at + s.j * P:at + (s.j + 1) * P],
                                      HT[:, k, s.b, s.blk * BLOCK:(s.blk + 1) * BLOCK], start=k == 0, stop=k == KF - 1)
                        last.then_inc(full, 1)
                elif s.kind == "down":
                    pe.wait_ge(w_in["w2"], 16 * (s.l + 1))
                    pe.wait_ge(b_evac, s.hid_b)
                    if LAYERS[s.l]["act"] == "swiglu":
                        pe.wait_ge(a_evac, s.hid_a)
                    ps = need_a(s.an)
                    for t in range(2):
                        tok = (s.u * 2 + t) * P
                        for k in range(HIDDEN // P):
                            last = mm(ps[:, t * FEAT:(t + 1) * FEAT], HID[s.par][:, k, tok:tok + P], W2[:, k, :],
                                      start=k == 0, stop=k == HIDDEN // P - 1)
                    last.then_inc(a_full, 1)

        @block.scalar
        def _(act):
            def from_b(n):
                act.wait_ge(b_full, n + 1)
                return PB[:, n % B_SLOTS, :]

            f = nc.scalar.activation
            act.wait_ge(consts_in, 16 * 7)
            f(COND[:, 1], COND[:, 0], ACT.Silu).then_inc(cond_ready, 1)
            act.wait_ge(mod_ready, 1)
            for s in steps:
                if s.kind == "stats":
                    act.wait_ge(stats_ready, s.stats + 1)
                    f(RSTD[:, s.b, :], MV[:, s.b, :, 1], ACT.Sqrt).then_inc(rstd_ready, 1)
                elif s.kind == "norm":
                    for kf in range(KF):
                        ps = from_b(s.b0 + kf)
                        has = (s.l, s.i) in NORMS
                        kw = dict(scale=MODC[:, mod_col(s.l, s.i, 0, kf), s.b:s.b + 1],
                                  bias=MODC[:, mod_col(s.l, s.i, 1, kf), s.b:s.b + 1]) if has else {}
                        lo = s.blk * BLOCK
                        cuts = [(0, BLOCK, lo)]
                        if s.i == 0 and LAYERS[s.l]["kind"] == "window":
                            cuts = [(0, SHIFT, TOKENS - SHIFT), (SHIFT, BLOCK, 0)] if s.blk == 0 else \
                                [(0, BLOCK, lo - SHIFT)]
                        for a, z, at in cuts:
                            last = f(HT[:, kf, s.b, at:at + z - a], ps[:, a:z], ACT.Identity, **kw)
                        last.then_inc(b_evac, 1)
                elif s.kind == "context_norm" and s.b0 is not None:
                    act.wait_ge(stats_ready, s.stats + 1)
                    f(RSTD[0:CTX, 0, 0:BATCH], MV[0:CTX, 0, 0:BATCH, 1], ACT.Sqrt).then_inc(rstd_ready, 1)
                    for kf in range(KF):
                        f(CTN[:, kf, :], from_b(s.b0 + kf)[:, 0:BATCH * CTX], ACT.Copy).then_inc(b_evac, 1)
                elif s.kind == "project":
                    ps = from_b(s.bn)
                    if s.split >= 2:
                        act.wait_ge(split_done, s.split - 1)
                    col = {"q": 4 if s.cross else 0, "k": 2, "ck": 6}[s.which] + s.hh
                    f(RAW[:, s.split % 2, 0:s.width], ps[:, 0:s.width], ACT.Identity,
                      bias=COLS[:, s.l, col:col + 1], scale=0.25 if s.which == "q" else 1.0).then_inc(b_evac, 1)
                elif s.kind == "max":
                    ps = from_b(s.g.max_b)
                    if s.m >= 2:
                        act.wait_ge(max_split, s.m - 1)
                    f(NT[:, s.m % 2, :], ps[0:GROUP * TILES, 0:P], ACT.Copy, scale=-1.0).then_inc(b_evac, 1)
                elif s.kind == "scores":
                    s, h0, bn = s.of, s.h0, s.bn
                    n = keys_of(s.g)
                    for h in (h0, h0 + 1):
                        ps = from_b(bn + h - h0)
                        if s.pv >= 2:
                            act.wait_ge(pv_done, s.pv - 1)
                        kw = dict(bias=MCOL[:, s.g.b:s.g.b + 1]) if s.g.cross and LAYERS[s.g.l]["mask"] else {}
                        f(PT[0:n, s.pv % 2, h, :], ps[0:n, :], ACT.Exp, **kw).then_inc(b_evac, 1)
                elif s.kind == "topk_turn":
                    k = s.of
                    act.wait_ge(tk_arg, k.n + 1)
                    f(EP, EP, ACT.Exp).then_inc(tk_exp, 1)
                    if k.of.pv >= 2:
                        act.wait_ge(pv_done, k.of.pv - 1)
                    for t in range(2):
                        ps = from_b(k.bn + t)
                        at = (k.t * 2 + t) * P
                        f(PT[0:CTX, k.of.pv % 2, :, at:at + P], ps[0:CTX, :].rearrange("p (h t) -> p h t", h=GROUP),
                          ACT.Copy).then_inc(b_evac, 1)
                elif s.kind == "out_stage":
                    s = s.of
                    act.wait_ge(pv_done, s.pv + 1)
                    if s.ost >= 2:
                        act.wait_ge(ost_out[s.ost % 2], 16 * (s.ost // 2))
                    f(OST[:, s.ost % 2, :], PC[:, :], ACT.Copy).then_inc(c_evac, 1)
                elif s.kind == "up":
                    ps = from_b(s.bn)
                    fn = {"tanh": ACT.Gelu_apprx_tanh, "erf": ACT.Gelu, "swiglu": ACT.Silu}[LAYERS[s.l]["act"]]
                    f(HID[s.par][:, s.j, :], ps, fn, bias=COLS[:, s.l, 8 + s.j:9 + s.j]).then_inc(b_evac, 1)

        @block.vector
        def _(dve):
            chain = [0]

            def link(ins_):
                chain[0] += 1
                ins_.then_inc(dve_step, 1)
                dve.wait_ge(dve_step, chain[0])

            def from_a(n):
                dve.wait_ge(a_full, n + 1)
                return PA[:, n % A_SLOTS, :]

            v = nc.vector

            def variance(var, eps):
                v.tensor_scalar(var, var, eps, None, ALU.add).then_inc(stats_ready, 1)

            def rstd(y, var, t, n):
                dve.wait_ge(rstd_ready, n + 1)
                link(v.reciprocal(y, y))
                link(v.tensor_tensor(t, y, y, ALU.mult))
                link(v.tensor_tensor(t, t, var, ALU.mult))
                link(v.tensor_scalar(t, t, -0.5, 1.5, ALU.mult, ALU.add))
                link(v.tensor_tensor(y, y, t, ALU.mult))

            v.memset(VA[:], 1.0).then_inc(setup_dve, 1)
            v.memset(ONE, 1.0).then_inc(setup_dve, 1)
            dve.wait_ge(consts_in, 16 * 7)
            link(v.tensor_copy(IDB[:], IDF[:]))
            link(v.tensor_scalar(COLS[:, :, 0:2], COLS[:, :, 0:2], 0.25, None, ALU.mult))
            link(v.tensor_scalar(COLS[:, :, 4:6], COLS[:, :, 4:6], 0.25, None, ALU.mult))
            dve.wait_ge(a_full, 1)
            ps = PA[:, 0, 0:NCOLS * BATCH].rearrange("p (c b) -> p c b", b=BATCH)
            for b in range(BATCH):
                last = v.tensor_tensor(MODC[:, :, b], ps[:, :, b], MODB[:, 0, :], ALU.add)
            last.then_inc(a_evac, 1)
            dve.wait_ge(a_evac, 1)
            for b in range(BATCH):
                m = MODC[:, :, b].rearrange("p (e s k) -> p e s k", s=2, k=KF)[:, :, 0, :]
                w = MODB[:, 1, :].rearrange("p (e s k) -> p e s k", s=2, k=KF)[:, :, 0, :]
                last = v.scalar_tensor_tensor(out=m, in0=m, scalar=1.0, in1=w, op0=ALU.add, op1=ALU.mult)
            last.then_inc(mod_ready, 1)
            dve.wait_ge(mask_ready, 4)
            n_rows = 0
            for s in steps:
                if s.kind == "stats":
                    dve.wait_ge(x_in, 32)
                    if s.xadd:
                        dve.wait_ge(x_add, s.xadd)
                    for t in range(TILES):
                        last = v.bn_stats(STAT[:, t, :], X[:, s.b * TILES + t, :])
                    link(last)
                    for t in range(TILES):
                        last = v.bn_aggr(MV[:, s.b, t, :], STAT[:, t, :])
                    link(last)
                    variance(MV[:, s.b, :, 1], LAYERS[s.l]["eps"])
                    rstd(RSTD[:, s.b, :], MV[:, s.b, :, 1], STAT[:, :, 0], s.stats)
                elif s.kind == "norm":
                    if s.xn >= 2:
                        dve.wait_ge(b_full, s.xn_b)
                    for t in range(4):
                        tile = s.blk * 4 + t
                        last = v.tensor_scalar(XN[:, s.xn % 2, t, :], X[:, s.b * TILES + tile, :],
                                               MV[:, s.b, tile, 0:1], RSTD[:, s.b, tile:tile + 1],
                                               ALU.subtract, ALU.mult)
                    last.then_inc(xn_ready, 1)
                elif s.kind == "context_norm" and s.b0 is not None:
                    dve.wait_ge(w_in["misc"], 16)
                    for b in range(BATCH):
                        last = v.bn_stats(STAT[0:CTX, b, :], CTOK[:, b, :])
                    link(last)
                    for b in range(BATCH):
                        last = v.bn_aggr(MV[0:CTX, 0, b, :], STAT[0:CTX, b, :])
                    link(last)
                    variance(MV[0:CTX, 0, 0:BATCH, 1], LAYERS[s.l]["eps"])
                    rstd(RSTD[0:CTX, 0, 0:BATCH], MV[0:CTX, 0, 0:BATCH, 1], STAT[0:CTX, 0:BATCH, 0], s.stats)
                    for b in range(BATCH):
                        last = v.tensor_scalar(CNRM[:, b, :], CTOK[:, b, :], MV[0:CTX, 0, b, 0:1],
                                               RSTD[0:CTX, 0, b:b + 1], ALU.subtract, ALU.mult)
                    last.then_inc(xn_ready, 1)
                elif s.kind == "gate":
                    n_rows += 3
                    dve.wait_ge(w_in["rows"], 16 * n_rows)
                    if s.an is not None:
                        ps = from_a(s.an)[:, 0:BATCH * FEAT].rearrange("p (b f) -> p b f", b=BATCH)
                        v.tensor_tensor(GB[:, :, 0, :], ps, bcast(BB[:, 0, :], BATCH), ALU.add).then_inc(a_evac, 1)
                        dve.wait_ge(a_evac, s.an + 1)
                        v.tensor_tensor(GB[:, :, 1, :], GB[:, :, 0, :], bcast(BB[:, 1, :], BATCH), ALU.mult)\
                            .then_inc(gate_ready, 1)
                elif s.kind == "rotate":
                    s = s.of
                    if s.l == 3:
                        dve.wait_ge(w_in["rope3"], 16)
                    ps = from_a(s.an)
                    if s.split:
                        dve.wait_ge(split_done, s.split)
                    v.tensor_tensor(tok_view(ROT, s), tok_view(ps, s), rope_cols(s, 1), ALU.mult).then_inc(a_evac, 1)
                elif s.kind in ("v", "ctx_v"):
                    ps = from_a(s.an)
                    i = int(s.kind == "ctx_v")
                    n = CTX if i else P
                    tiles = slice(s.b, s.b + 1) if i else slice(s.u * 4, s.u * 4 + 4)
                    nt = 1 if i else 4
                    dst = VA[0:n, tiles, :, 0:HEAD]
                    src = ps[0:n, 0:nt * FEAT].rearrange("p (t h d) -> p t h d", t=nt, h=HEADS)
                    for t in range(nt):
                        bias = BB[0:n, 2, :].rearrange("p (h d) -> p h d", h=HEADS)
                        last = v.tensor_tensor(dst[:, t], src[:, t], bias, ALU.add)
                    last.then_inc(a_evac, 1)
                elif s.kind == "first":
                    g = s.g
                    ps = from_a(s.an)
                    if g.akind == "full" and LAYERS[g.l]["mask"]:
                        dve.wait_ge(mask_ready, 4)
                        h, t = s.u // TILES, s.u % TILES
                        dve.wait_ge(a_evac, s.an)
                        v.tensor_tensor_reduce(out=JUNK[:], in0=ps, in1=MASKQ[:, t, :], scale=1.0, scalar=-3.4e38,
                                               op0=ALU.add, op1=ALU.max, accum_out=NM[:, g.m % 2, s.u:s.u + 1])\
                            .then_inc(a_evac, 1)
                    elif g.akind == "full":
                        v.tensor_reduce(NM[:, g.m % 2, s.u:s.u + 1], ps, AX.X, ALU.max).then_inc(a_evac, 1)
                    elif g.akind == "window":
                        v.tensor_reduce(NM[:, g.m % 2, s.u * TILES:(s.u + 1) * TILES],
                                        ps.rearrange("p (w k) -> p w k", k=P), AX.X, ALU.max).then_inc(a_evac, 1)
                    else:
                        o = NM[:, g.m % 2, :].rearrange("p (h q) -> p q h", h=GROUP)
                        i_ = ps.rearrange("p (q h k) -> p q h k", q=2, k=P)
                        for t in range(2):
                            last = v.tensor_reduce(o[:, 2 * s.u + t, :], i_[:, t, 0:GROUP, 0:CTX], AX.X, ALU.max)
                        last.then_inc(a_evac, 1)
                elif s.kind == "topk":
                    p2 = s.n % 2
                    ps = from_a(s.an).rearrange("p (q h k) -> p q h k", q=2, k=P)
                    if s.n >= 2:
                        dve.wait_ge(tk_arg, s.n - 1)
                    for t in range(2):
                        last = v.tensor_copy(TS[:, p2, t * GROUP:(t + 1) * GROUP, :], ps[:, t, 0:GROUP, 0:CTX])
                    last.then_inc(a_evac, 1)
                    dve.wait_ge(a_evac, s.an + 1)
                    for i in range(8):
                        last = v.max(M8[:, p2, i, :], TS[:, p2, i, :])
                    link(last)
                    for i in range(8):
                        last = v.match_replace(S3[:, p2, i, :], M8[:, p2, i, :], TS[:, p2, i, :], GONE)
                    link(last)
                    for i in range(8):
                        last = v.max(M8B[:, i, :], S3[:, p2, i, :])
                    link(last)
                    for i in range(8):
                        last = v.match_replace(S3[:, p2, i, :], M8B[:, i, :], S3[:, p2, i, :], GONE)
                    last.then_inc(tk_sel, 1)
                    dve.wait_ge(tk_sel, s.n + 1)
                elif s.kind == "normalise":
                    s = s.of
                    dve.wait_ge(od_in, s.need)
                    link(v.reciprocal(DEN[:], DEN[:]))
                    v.tensor_tensor(HT[:, s.hh, s.b, :], HT[:, s.hh, s.b, :], DEN[:], ALU.mult).then_inc(norm_done, 1)
                elif s.kind in ("out", "down"):
                    i = 2 if s.kind == "down" else int(s.cross)
                    ps = from_a(s.an)[:, 0:2 * FEAT].rearrange("p (t f) -> p t f", t=2)
                    if s.xadd:
                        dve.wait_ge(x_add, s.xadd)
                    if LAYERS[s.l]["gates"][i] is not None:
                        v.tensor_tensor(TMP[:], ps, bcast(GB[:, s.b, 0, :], 2), ALU.mult).then_inc(a_evac, 1)
                    else:
                        v.tensor_tensor(TMP[:], ps, bcast(BB[:, 1, :], 2), ALU.add).then_inc(a_evac, 1)
                elif s.kind == "up" and s.an is not None:
                    ps = from_a(s.an)
                    dve.wait_ge(b_evac, s.bn + 1)
                    v.scalar_tensor_tensor(out=HID[s.par][:, s.j, :], in0=ps[:, 0:BLOCK],
                                           scalar=COLS[:, s.l, 16 + s.j:17 + s.j], in1=HID[s.par][:, s.j, :],
                                           op0=ALU.add, op1=ALU.mult).then_inc(a_evac, 1)

        @block.gpsimd
        def _(pool):
            chain = [0]

            def link(ins_):
                chain[0] += 1
                ins_.then_inc(pool_step, 1)
                pool.wait_ge(pool_step, chain[0])

            g_ = nc.gpsimd
            pool.wait_ge(mask_in, 64)
            raw = PT[:, :, :, :].rearrange("p s h t -> p (s h t)")
            for n, (dst, src) in enumerate(((MASKT, raw[:, 0:2048].bitcast(u8).rearrange("p (t q) -> p t q", t=TILES)),
                             (MASKQ, raw[:, 2048:4096].bitcast(u8).rearrange("p (t q) -> p t q", t=TILES)),
                             (MROW.rearrange("p b t -> p (b t)"), JUNK[0:1, 0:BATCH * CTX // 2].bitcast(u8)),
                             (MCOL[:], JUNK[0:CTX, 512:512 + BATCH // 2].bitcast(u8)))):
                (g_.tensor_scalar(dst, src, -1.0, -NEG, ALU.add, ALU.mult)
                 .then_inc(mask_ready, 1))
                pool.wait_ge(mask_ready, n + 1)
            pool.wait_ge(a_evac, 1)
            g_.memset(K6[PARTS:P, :, :, :], 1.0).then_inc(k_ones, 1)
            pool.wait_ge(k_ones, 1)
            for s in steps:
                if s.kind == "gate":
                    if s.l == 2 and s.i == 2:
                        g_.memset(K6[PARTS:P, 2, :, :], 1.0).then_inc(k_ones, 1)
                        pool.wait_ge(k_ones, 2)
                elif s.kind == "split":
                    s = s.of
                    buf = s.which[-1]
                    r = RAW[:, s.split % 2, 0:s.width]
                    pool.wait_ge(b_evac, s.bn + 1)
                    if s.rope:
                        pool.wait_ge(a_evac, s.an + 1)
                        rv = tok_view(RAW[:, s.split % 2, :], s)
                        link(g_.tensor_tensor(out=rv, in0=rv, in1=rope_cols(s, 0), op=ALU.mult))
                        link(g_.tensor_tensor(out=r, in0=r, in1=ROT[:, 0:s.width], op=ALU.add))
                    if s.written:
                        pool.wait_ge(scr_in[buf], 96 * s.written)
                    parts = SPLIT[buf][:, :, s.blk * BLOCK:s.blk * BLOCK + s.width]
                    link(g_.tensor_copy(parts[:, 0, :], r))
                    link(g_.tensor_tensor(out=r, in0=r, in1=parts[:, 0, :], op=ALU.subtract))
                    link(g_.tensor_copy(parts[:, 1, :], r))
                    g_.tensor_tensor(out=parts[:, 2, :], in0=r, in1=parts[:, 1, :], op=ALU.subtract)\
                        .then_inc(split_done, 1)
                    pool.wait_ge(split_done, s.split + 1)
                elif s.kind == "max":
                    p2 = s.m % 2
                    pool.wait_ge(b_evac, s.g.max_b + 1)
                    if s.m >= 2:
                        pool.wait_ge(mx_out, 16 * (s.m - 1))
                    r, parts = NT[:, p2, :], MS[:, p2]
                    link(g_.tensor_copy(parts[:, 0, :], r))
                    link(g_.tensor_tensor(out=r, in0=r, in1=parts[:, 0, :], op=ALU.subtract))
                    link(g_.tensor_copy(parts[:, 1, :], r))
                    g_.tensor_tensor(out=parts[:, 2, :], in0=r, in1=parts[:, 1, :], op=ALU.subtract)\
                        .then_inc(max_split, 1)
                    pool.wait_ge(max_split, s.m + 1)
                elif s.kind == "topk":
                    p2 = s.n % 2
                    pool.wait_ge(tk_sel, s.n + 1)
                    link(g_.tensor_scalar(S3[:, p2], S3[:, p2], GONE * 0.9, -1.0e30, ALU.is_gt, ALU.mult))
                    if s.n:
                        pool.wait_ge(b_full, s.ep_b)
                    m = M8[:, p2, :, 0:1].broadcast_to([P, 8, CTX])
                    link(g_.tensor_tensor(out=EP, in0=TS[:, p2], in1=m, op=ALU.subtract))
                    g_.tensor_tensor(out=EP, in0=EP, in1=S3[:, p2], op=ALU.add).then_inc(tk_arg, 1)
                    pool.wait_ge(tk_arg, s.n + 1)
                elif s.kind in ("out", "down"):
                    i = 2 if s.kind == "down" else int(s.cross)
                    pool.wait_ge(a_evac, s.an + 1)
                    if LAYERS[s.l]["gates"][i] is not None:
                        pool.wait_ge(gate_ready, s.gate)
                        link(g_.tensor_tensor(out=TMP[:], in0=TMP[:], in1=bcast(GB[:, s.b, 1, :], 2), op=ALU.add))
                    t0 = s.b * TILES + (s.blk * 4 if s.kind == "down" else 0) + s.u * 2
                    g_.tensor_tensor(out=X[:, t0:t0 + 2, :], in0=X[:, t0:t0 + 2, :], in1=TMP[:], op=ALU.add)\
                        .then_inc(x_add, 1)
                    pool.wait_ge(x_add, s.xadd + 1)


def kernel(**inputs):
    import concourse.bacc as bacc
    from concourse.bass_utils import run_bass_kernel_spmd

    a = {k: np.asarray(v) for k, v in inputs.items()}
    zeros = np.zeros
    f32 = np.float32

    def cols(v):
        return v.reshape(-1, P).T

    def rope_table(n, repeat):
        inv = 1.0 / 10000.0 ** (np.arange(0, HEAD, 2, dtype=f32) / f32(HEAD))
        ang = np.outer(np.concatenate([inv, inv]), np.arange(n, dtype=f32)).astype(f32)
        sign = np.concatenate([-np.ones(HEAD // 2), np.ones(HEAD // 2)])[:, None]
        return np.stack([np.tile(np.cos(ang), (8, 1)), np.tile(np.sin(ang) * sign, (8, 1))], 1).astype(f32)

    rot = zeros((P, P), f32)
    for o in range(P):
        rot[(o // HEAD) * HEAD + (o % HEAD + HEAD // 2) % HEAD, o] = 1.0

    L = {l: (lambda n, l=l: a[f"L{l}_xcond_{n}"]) for l in range(4)}
    z256 = zeros(FEAT, f32)
    d = {
        "x": a["x"], "ctx": a["ctx_1024"],
        "ctxt": a["ctx_1024"].transpose(2, 0, 1).reshape(KF, P, BATCH * CTX).transpose(1, 0, 2),
        "cond": a["cond_1024"].T.reshape(KF, P, BATCH).transpose(1, 0, 2),
        "mask_q": a["mask_SxS_bk0"], "mask_t": a["mask_SxS_bk0"].T,
        "kv_row": a["mask_BxS2_bf1"].reshape(1, BATCH * CTX),
        "kv_col": a["mask_BxS2_bf1"].T,
        "ident": np.eye(P, dtype=f32), "rotm": rot,
        "rope0": rope_table(512, 8).reshape(P, -1), "rope3": rope_table(1024, 8).reshape(P, -1),
        "mod_0": L[0]("adaLN_W"), "mod_1": L[1]("W_mod"), "mod_2": L[2]("w_ada"),
    }
    mod_bias = {0: L[0]("adaLN_b"), 1: L[1]("b_mod"), 2: L[2]("b_ada")}
    norm_w = {0: [L[0]("norm1_w"), L[0]("normc_w"), L[0]("norm2_w")]}
    mb, mw = [], []
    for l, i in NORMS:
        if l == 3:
            d[f"mod_{l}_{i}"] = L[3](f"ln{i + 1}_w").T
        for s in range(2):
            c = LAYERS[l]["norms"][i][s]
            bias = L[3](f"ln{i + 1}_b") if l == 3 else mod_bias[l]
            mb.append(cols(bias[c * FEAT:(c + 1) * FEAT]))
            mw.append(cols(norm_w[0][i]) if l == 0 and s == 0 else np.ones((P, KF), f32))
    d["modb"] = np.stack([np.concatenate(mb, 1), np.concatenate(mw, 1)], 1)

    cat = np.concatenate
    d.update({
        "qkv_0": L[0]("qkv_W"), "qkv_1": L[1]("W_qkv"), "qkv_2": L[2]("w_qkv"), "qkv_3": L[3]("qkv_w").T,
        "o_0": L[0]("attn_out_W"), "o_1": L[1]("W_proj"), "o_2": L[2]("w_so"), "o_3": L[3]("sa_out_w").T,
        "cq_0": L[0]("cq_W"), "cq_1": L[1]("W_qc"), "cq_2": L[2]("w_q"), "cq_3": L[3]("q_w").T,
        "ckv_0": cat([L[0]("ck_W"), L[0]("cv_W")], 1), "ckv_1": L[1]("W_kvc"), "ckv_2": L[2]("w_kv"),
        "ckv_3": cat([L[3]("k_w").T, L[3]("v_w").T], 1),
        "co_0": L[0]("co_W"), "co_1": L[1]("W_cproj"), "co_2": L[2]("w_co"), "co_3": L[3]("ca_out_w").T,
        "w1_0": L[0]("mlp_W1"), "w1_1": L[1]("W_mlp1"), "w1_2": L[2]("w_m1"), "w1_3": L[3]("ffn_w1").T,
        "w2_0": L[0]("mlp_W2"), "w2_1": L[1]("W_mlp2"), "w2_2": L[2]("w_m2"), "w2_3": L[3]("ffn_w2").T,
    })
    qkv_b = {1: L[1]("b_qkv"), 2: L[2]("b_qkv")}
    cq_b = {1: L[1]("b_qc"), 2: L[2]("b_q")}
    ckv_b = {1: L[1]("b_kvc"), 2: L[2]("b_kv")}
    b1 = {0: L[0]("mlp_b1"), 1: L[1]("b_mlp1"), 2: L[2]("b_m1"), 3: L[3]("ffn_b1")}
    out_b = {(0, 2): L[0]("mlp_b2"), (1, 0): L[1]("b_proj"), (1, 1): L[1]("b_cproj"), (1, 2): L[1]("b_mlp2"),
             (2, 0): L[2]("b_so"), (2, 1): L[2]("b_co"), (2, 2): L[2]("b_m2"), (3, 2): L[3]("ffn_b2")}
    table = zeros((P, 4, 24), f32)
    for l in range(4):
        if l in qkv_b:
            table[:, l, 0:4] = cols(qkv_b[l][0:2 * FEAT])
            table[:, l, 4:6] = cols(cq_b[l])
            table[:, l, 6:8] = cols(ckv_b[l][0:FEAT])
        table[:, l, 8:8 + len(b1[l]) // P] = cols(b1[l])
        for i in range(3):
            c = LAYERS[l]["gates"][i]
            d[f"gb_{l}_{i}"] = mod_bias[l][c * FEAT:(c + 1) * FEAT] if c is not None else z256
            d[f"ob_{l}_{i}"] = out_b.get((l, i), z256)
            d[f"vb_{l}_{i}"] = z256
        if l in qkv_b:
            d[f"vb_{l}_0"] = qkv_b[l][2 * FEAT:]
            d[f"vb_{l}_1"] = ckv_b[l][FEAT:]
    d["cols"] = table

    nc = bacc.Bacc("TRN2", target_bir_lowering=False, num_devices=1)
    arrays, aps = {}, {}
    for name, v in d.items():
        v = np.ascontiguousarray(v)
        arrays["in_" + name] = v
        aps[name] = nc.dram_tensor("in_" + name, v.shape, mybir.dt.from_np(v.dtype), kind="ExternalInput").ap()
    out = nc.dram_tensor("out_x", (BATCH, TOKENS, FEAT), mybir.dt.float32, kind="ExternalOutput").ap()
    blocks_kernel(nc, aps, out)
    r = run_bass_kernel_spmd(nc, [arrays], core_ids=[0])
    return r.results[0]["out_x"]
```

```python
from contextlib import ExitStack

import numpy as np
import concourse.bass as bass
from concourse import mybir

BATCH, TOKENS, FEAT = 2, 1024, 256
HEADS, HEAD = 16, 16
CTX = 77
HIDDEN = 1024
TOPK = 16
WINDOW, SHIFT = 128, 64
P = 128
KF = FEAT // P
TILES = TOKENS // P
GROUP = 4
GROUPS = HEADS // GROUP
BLOCK = 512
BLOCKS = TOKENS // BLOCK
PARTS = 6 * HEAD
ROWS = PARTS + 3
PART_OF = {"q": (0, 0, 0, 1, 1, 2), "k": (0, 1, 2, 0, 1, 0)}
VCOLS = 2 * HEAD
A_SLOTS, B_SLOTS, RING = 2, 3, 3
LEAD = 10
NEG = -float(2.0 ** 100)
GONE = -3.0e38

LAYERS = [
    dict(name="L0", eps=1e-5, rope=512, cross_rope=0, mask=True, kind="full", silu_cond=False, act="tanh",
         mod=["adaLN_W"], gates=(2, 5, 8), norms=[(1, 0), (4, 3), (7, 6)]),
    dict(name="L1", eps=1e-6, rope=0, cross_rope=0, mask=False, kind="full", silu_cond=True, act="tanh",
         gates=(2, None, 5), norms=[(1, 0), None, (4, 3)]),
    dict(name="L2", eps=1e-6, rope=0, cross_rope=0, mask=False, kind="window", silu_cond=True, act="swiglu",
         gates=(2, 5, 8), norms=[(1, 0), (4, 3), (7, 6)]),
    dict(name="L3", eps=1e-5, rope=1024, cross_rope=1024, mask=False, kind="full", silu_cond=False, act="erf",
         gates=(None, None, None), norms=[(0, 1), (0, 1), (0, 1)]),
]
NORMS = [(l, i) for l, cfg in enumerate(LAYERS) for i in range(3) if cfg["norms"][i] is not None]
NCOLS = len(NORMS) * 2 * KF


class Step(dict):

    def __getattr__(self, name):
        return self[name]

    def __setattr__(self, name, value):
        self[name] = value


def plan():
    steps = []
    count = dict(m=0, a=1, b=0, c=0, split=0, pv=0, xn=0, xadd=0, group=0, q=0, k=0, od=0, gate=0,
                 ost=0, stats=0, topk=0, mid=0, sel=0)
    all_groups = []
    turned_topk = []
    projected = dict(q=0, k=0)
    turned = []
    added = [0] * BATCH
    maxima = [0] * RING
    filled = [0] * RING

    def take(kind, n=1):
        count[kind] += n
        return count[kind] - n

    def add(kind, **kw):
        s = Step(kind=kind, **kw)
        steps.append(s)
        return s

    def norm_steps(l, i, b):
        n = take("stats")
        add("stats", l=l, i=i, b=b, stats=n, xadd=added[b])
        for blk in range(BLOCKS):
            s = add("norm", l=l, i=i, b=b, blk=blk, b0=take("b", KF), xn=take("xn"), stats=n)
            turned.append(s.b0 + KF)
            s.xn_b = turned[-3] if len(turned) > 2 else 0
        return s.b0 + KF - 1

    def project(l, which, b, hh, blk, ht, rope, whiches_cross):
        s = add("project", l=l, which=which, b=b, hh=hh, blk=blk, ht=ht, bn=take("b"), rope=rope,
                split=take("split"), width=BLOCK, cross=whiches_cross,
                before=projected[which] // BLOCKS)
        projected[which] += 1
        return s

    def rotate(s):
        if s.rope:
            s.an = take("a")
            add("rotate", of=s)
        add("split", of=s)
        if s.blk == BLOCKS - 1:
            buf = s.which
            take(buf)
            add("scratch", of=s)

    def attention(l, cross, ht):
        cfg = LAYERS[l]
        kind = "cross" if cross else cfg["kind"]
        select = cross and cfg["kind"] == "window"
        direct = kind != "full"
        whiches = ("q",) if cross else ("q", "k")
        first, second = [], []
        groups = []
        for n in range(BATCH * GROUPS):
            g = Step(l=l, cross=cross, akind=kind, b=n // GROUPS, g=n % GROUPS, local=n, n=take("group"))
            g.select = select
            g.m = None if direct else take("m")
            g.slot = g.n % RING
            groups.append(g)
            all_groups.append(g)
        def projection_items(b, hh):
            return [("project", b, hh, w, blk) for w in whiches for blk in range(BLOCKS)]

        spread = {0: [(0, 1)], 1: [(1, 0)], 2: [(1, 1)]}
        first += projection_items(0, 0) + [("flush",), ("norm",)]
        for g in groups:
            first.append(("load", g))
            units = 0 if direct else GROUP * TILES
            items = [i for b, hh in spread.get(g.local, []) for i in projection_items(b, hh)]
            gap = max(1, units // len(items)) if items else 1
            for u in range(units):
                first.append(("first", g, u))
                if items and (u + 1) % gap == 0:
                    first.append(items.pop(0))
            first += items
            if g.local in spread:
                first.append(("flush",))
            if not direct:
                first.append(("max", g))
        for g in groups:
            if g.g == 0 and not cross:
                second.append(("v", g))
            keys = TILES if kind == "full" else 1
            for qh in range(BLOCKS):
                for kt in range(keys):
                    second.append(("second", g, qh, kt, kt == keys - 1))
            second.append(("end", g))
        pos = 0
        emitted = {}
        unsplit = []

        def do_first():
            nonlocal pos
            item = first[pos]
            pos += 1
            if item[0] == "project":
                _, b, hh, which, blk = item
                s = project(l, which, b, hh, blk, ht[b], cfg["cross_rope" if cross else "rope"], cross)
                if unsplit:
                    rotate(unsplit.pop())
                unsplit.append(s)
                return 0
            if item[0] == "flush":
                rotate(unsplit.pop())
                return 0
            if item[0] == "norm":
                ht.append(norm_steps(l, int(cross), 1))
                return 0
            if item[0] == "load":
                g = item[1]
                g.written = {w: count[w] for w in whiches}
                g.before = all_groups[g.n - RING] if g.n >= RING else None
                filled[g.slot] += len(whiches)
                g.filled = filled[g.slot]
                add("load", g=g)
                return 0
            if item[0] == "first":
                _, g, u = item
                add("first", g=g, u=u, an=take("a"))
                g.last_a = count["a"] - 1
                return 1
            g = item[1]
            g.max_b = take("b")
            maxima[g.slot] += 1
            g.max_filled = maxima[g.slot]
            add("max", g=g, m=g.m)
            emitted[g.n] = True
            return 0

        def run_first(units, until=None):
            nonlocal pos
            done = 0
            while pos < len(first):
                if until is not None:
                    if until in emitted:
                        return
                elif done >= units:
                    if first[pos][0] not in ("max", "project", "flush"):
                        return
                done += do_first()

        per_step = GROUP // BLOCKS
        if direct:
            while pos < len(first) and not (first[pos][0] == "load" and first[pos][1].local >= 2):
                do_first()
        else:
            run_first(0, until=groups[0].n)
            run_first(LEAD)
        vlast = count["a"] - 1
        pending = None
        late = []

        def tick():
            for item in list(late):
                item[0] -= 1
                if item[0] <= 0:
                    late.remove(item)
                    item[1]()

        def emit_pv():
            nonlocal pending
            if pending is None:
                return
            s = pending
            pending = None
            take("pv")
            if s.kt == 0:
                s.g.cn = take("c")
            s.cn = s.g.cn
            add("pv", of=s)
            if s.last:
                s.ost = take("ost")
                add("out_stage", of=s)

        def turn_topk():
            nonlocal pending
            k = unturned.pop(0)
            k.bn = take("b", 2)
            add("topk_turn", of=k)
            if k.t == TILES // BLOCKS // 2 - 1:
                k.of.last_b = count["b"] - 1
                pending = k.of
                emit_pv()
                if k.of.qh == BLOCKS - 1:
                    end_of(k.g)

        unturned = []
        units = []

        def end_of(g):
            g.ost_last = count["ost"] - 1
            g.pv_last = count["pv"] - 1
            if g.g % 2 == 1:
                out_of(g)

        def out_of(g):
            s = add("dense", l=l, b=g.b, hh=g.g // 2, n=take("od"), ost=g.ost_last, akind=kind)
            late.append([1, lambda: add("reciprocal", of=s)])
            late.append([3 if kind == "full" else 2, lambda: add("normalise", of=s)])
            if g.g == GROUPS - 1:
                def out():
                    for u in range(TILES // 2):
                        add("out", l=l, cross=cross, b=g.b, u=u, an=take("a"), od=count["od"], xadd=take("xadd"),
                            gate=gates_seen)
                        added[g.b] = count["xadd"]
                late.append([6 if kind == "full" else 3, out])

        for item in second:
            if item[0] == "v":
                g = item[1]
                while unturned:
                    turn_topk()
                emit_pv()
                for u in range(2):
                    add("v", l=l, b=g.b, u=u, an=take("a"), pv=count["pv"], ht=ht[g.b])
                    g.v_a = count["a"] - 1
                vlast = count["a"] - 1
            elif item[0] == "second":
                _, g, qh, kt, last = item
                if direct:
                    while qh == 0 and pos < len(first) and not (
                            first[pos][0] == "load" and first[pos][1].local > g.local + 2):
                        do_first()
                elif g.n not in emitted:
                    run_first(0, until=g.n)
                s = Step(g=g, qh=qh, kt=kt, last=last, v_a=vlast)
                if direct:
                    for t in range(TILES // BLOCKS // 2):
                        k = add("topk", of=s, g=g, qh=qh, t=t, an=take("a"), n=take("topk"),
                                sel=take("sel") if select else None)
                        units.append(k)
                        slots = 2 if select else 3
                        k.reuse = units[-slots - 1] if len(units) > slots else turned_topk[-1] if turned_topk else None
                        if len(unturned) == 2:
                            turn_topk()
                        unturned.append(k)
                else:
                    add("scores", of=s, h0=0, bn=take("b", 2))
                    run_first(per_step // 2)
                    add("scores", of=s, h0=2, bn=take("b", 2))
                    s.last_b = count["b"] - 1
                    run_first(per_step - per_step // 2)
                    emit_pv()
                s.pv = take("mid")
                if not direct:
                    pending = s
                tick()
            else:
                g = item[1]
                if not direct:
                    emit_pv()
                    end_of(g)
        while unturned:
            turn_topk()
        turned_topk.extend(units[-1:])
        while late:
            tick()

    gates_seen = 0
    for l, cfg in enumerate(LAYERS):
        ht = [norm_steps(l, 0, 0)]
        gates_seen += int(cfg["gates"][0] is not None)
        add("gate", l=l, i=0, an=take("a") if cfg["gates"][0] is not None else None, xadd=count["xadd"])
        attention(l, False, ht)
        ht = [norm_steps(l, 1, 0)]
        gates_seen += int(cfg["gates"][1] is not None)
        add("gate", l=l, i=1, an=take("a") if cfg["gates"][1] is not None else None, xadd=count["xadd"])
        if l == 1:
            c = add("context_norm", l=l, b0=take("b", KF), stats=take("stats"), xn=take("xn"))
            turned.append(c.b0 + KF)
        else:
            add("context_norm", l=l, b0=None)
        for hh in range(KF):
            s = add("project", l=l, which="ck", b=0, hh=hh, blk=0, ht=None, bn=take("b"), rope=cfg["cross_rope"],
                    split=take("split"), width=BATCH * CTX, cross=True,
                    before=projected["k"] // BLOCKS)
            projected["k"] += BLOCKS
            if s.rope:
                s.an = take("a")
                add("rotate", of=s)
            add("split", of=s)
            take("k")
            add("ctx_scratch", of=s)
        add("ctx_load", l=l, written=count["k"], pv=count["pv"])
        for b in range(BATCH):
            add("ctx_v", l=l, b=b, an=take("a"))
        attention(l, True, ht)
        ht = [norm_steps(l, 2, 0)]
        gates_seen += int(cfg["gates"][2] is not None)
        add("gate", l=l, i=2, an=take("a") if cfg["gates"][2] is not None else None, xadd=count["xadd"])
        pend = None

        def down(h):
            for u in range(BLOCK // P // 2):
                add("down", l=l, b=h.b, blk=h.blk, u=u, an=take("a"), xadd=take("xadd"), par=h.par,
                    hid_b=h.hid_b, hid_a=h.hid_a, gate=gates_seen)
                added[h.b] = count["xadd"]
            if l == len(LAYERS) - 1:
                add("store", b=h.b, blk=h.blk, xadd=count["xadd"])
        for blk in range(BATCH * BLOCKS):
            h = Step(b=blk // BLOCKS, blk=blk % BLOCKS, par=blk % 2, n=blk)
            for j in range(HIDDEN // P):
                s = add("up", l=l, b=h.b, blk=h.blk, j=j, bn=take("b"), par=h.par, n=h.n, ht=ht[h.b],
                        an=take("a") if cfg["act"] == "swiglu" else None)
            h.hid_b, h.hid_a = count["b"], count["a"]
            if blk == 0:
                ht.append(norm_steps(l, 2, 1))
            if pend is not None:
                down(pend)
            pend = h
        down(pend)
    return steps, count


def blocks_kernel(nc, ins, out):
    f32, bf16, u8 = mybir.dt.float32, mybir.dt.bfloat16, mybir.dt.uint8
    ALU, ACT, AX = mybir.AluOpType, mybir.ActivationFunctionType, mybir.AxisListType
    steps, total = plan()
    ctx = ExitStack()
    with ctx:
        def sb(name, shape, dt=f32):
            return ctx.enter_context(nc.sbuf_tensor(name, shape, dt))

        def sem(name):
            return ctx.enter_context(nc.semaphore(name))

        X = sb("x_tok", [P, BATCH * TILES, FEAT])
        HT = sb("h_feat", [P, KF, BATCH, TOKENS])
        RINGS = sb("rings", [P, 2, RING * GROUP * TOKENS // 2])
        Q6 = RINGS[:, 0, :].bitcast(bf16).rearrange("p (s h t) -> p s h t", s=RING, h=GROUP)
        K6 = RINGS[:, 1, :].bitcast(bf16).rearrange("p (s h t) -> p s h t", s=RING, h=GROUP)
        KC = RINGS[:, 1, :].bitcast(bf16).rearrange("p (s t) -> p s t", s=RING)[:, :, 0:HEADS * 80]\
            .rearrange("p s (h t) -> p s h t", t=80)
        WORK = sb("work", [P, 5120])
        RAW = WORK[:, 0:1024].rearrange("p (s t) -> p s t", s=2)
        ROT = WORK[:, 1024:1536]
        CTN = WORK[:, 1536:1536 + KF * BATCH * CTX].rearrange("p (k t) -> p k t", k=KF)
        SPLIT = {w: WORK[:, o:o + 1536].bitcast(bf16).rearrange("p (j t) -> p j t", j=3)
                 for w, o in (("q", 2048), ("k", 3584))}
        HID = [RINGS[:, 0, 0:4096].rearrange("p (j t) -> p j t", j=HIDDEN // P),
               WORK[:, 0:4096].rearrange("p (j t) -> p j t", j=HIDDEN // P)]
        VA = sb("v_and_ones", [P, TILES, HEADS, VCOLS])
        PT = sb("probs", [P, 2, GROUP, BLOCK])
        XN = PT[:, 0, :, :].rearrange("p (s c) t -> p s (c t)", s=2).rearrange("p s (c t) -> p s c t", t=FEAT)
        OST = sb("out_stage", [P, 2, BLOCK])
        DEN = sb("denominators", [P, TOKENS])
        GW = DEN[:, 0:KF * FEAT].rearrange("p (k f) -> p k f", k=KF)
        WR = sb("w_mlp", [P, 8192])
        MASKT = WR[:, 0:4096].bitcast(bf16).rearrange("p (t q) -> p t q", t=TILES)
        MASKQ = WR[:, 4096:8192].bitcast(bf16).rearrange("p (t q) -> p t q", t=TILES)
        W2 = WR[:, 4096:6144].rearrange("p (k f) -> p k f", k=HIDDEN // P)
        ROPE_L3 = WR[:, 6144:8192].rearrange("p (c t) -> p c t", c=2)
        NSC = 2 * GROUP * CTX
        TS = WR[:, 6144:6144 + 2 * NSC].rearrange("p (s i k) -> p s i k", s=2, k=CTX)
        EX = RINGS[:, 1, 4096:4096 + 3 * NSC].rearrange("p (s i k) -> p s i k", s=3, k=CTX)
        EW = WR[:, 0:3072].rearrange("p (s k) -> p s k", s=3)
        S3 = RINGS[:, 1, 4096:4096 + 2 * NSC].rearrange("p (s i k) -> p s i k", s=2, k=CTX)
        EP = [m.rearrange("p (i k) -> p i k", k=CTX) for m in
              (WR[:, 6144 + 2 * NSC:6144 + 3 * NSC], RINGS[:, 1, 4096 + 2 * NSC:4096 + 3 * NSC])]
        WQKV = sb("w_qkv", [P, KF, 3 * FEAT])
        WO = sb("w_out", [P, KF, FEAT])
        WCQ = sb("w_cross_q", [P, KF, FEAT])
        WCKV = sb("w_cross_kv", [P, KF, 2 * FEAT])
        MISC = sb("rope0_or_context", [P, 1024])
        ROPE_L0 = MISC[:, :].rearrange("p (c t) -> p c t", c=2)
        CTOK = MISC[0:CTX, 0:512].rearrange("p (b f) -> p b f", b=BATCH)
        CNRM = MISC[0:CTX, 512:1024].rearrange("p (b f) -> p b f", b=BATCH)
        GB = sb("gates", [P, BATCH, 2, FEAT])
        TMP = sb("branch_out", [P, 2, FEAT])
        BB = sb("row_biases", [P, 3, FEAT])
        CTXT = sb("ctx_feat", [P, KF, BATCH * CTX])
        IDF = sb("ident_f", [P, P])
        IDB = sb("ident_b", [P, P], bf16)
        ROTM = sb("rot_matrix", [P, P])
        COND = sb("cond", [P, 2, KF, BATCH])
        MODC = sb("mod_cols", [P, NCOLS, BATCH])
        MODB = sb("mod_bias_and_weight", [P, 2, NCOLS])
        COLS = sb("bias_cols", [P, 4, 24])
        STAT = sb("bn_stats", [P, TILES, 6])
        MV = sb("mean_var", [P, BATCH, TILES, 2])
        RSTD = sb("rstd", [P, BATCH, TILES])
        NM = sb("row_max", [P, 2, GROUP * TILES])
        NT = sb("neg_max", [GROUP * TILES, 2, P])
        MS = sb("neg_max_parts", [GROUP * TILES, 2, 3, P], bf16)
        JUNK = sb("masked_scores", [P, TOKENS], bf16)
        M8 = WORK[:, 1848:1976].rearrange("p (s i k) -> p s i k", s=2, k=8)
        M8B = WORK[:, 1976:2040].rearrange("p (i k) -> p i k", k=8)
        MROW = WORK[0:1, 1848:1848 + CTX].bitcast(bf16).rearrange("p (b t) -> p b t", b=BATCH)
        MCOL = sb("kv_mask_col", [CTX, BATCH])
        ONE = WORK[0:1, 1928:1928 + P // 2].bitcast(bf16)

        PA = ctx.enter_context(nc.psum_tensor("ring_a", [P, A_SLOTS, 1024], f32))
        PB = ctx.enter_context(nc.psum_tensor("ring_b", [P, B_SLOTS, BLOCK], f32))
        PC = ctx.enter_context(nc.psum_tensor("ring_c", [P, BLOCK], f32))

        QK_SCR = {w: nc.dram_tensor(f"scr_{w}", [BATCH, HEADS, 6, HEAD, TOKENS], bf16, kind="Internal").ap()
                  for w in "qk"}
        KC_SCR = nc.dram_tensor("scr_ctx_k", [HEADS, 6, HEAD, BATCH * CTX], bf16, kind="Internal").ap()
        MX_SCR = nc.dram_tensor("scr_max", [2, 3, GROUP * TILES, P], bf16, kind="Internal").ap()
        R_SCR = nc.dram_tensor("scr_recip", [2, 8, TOKENS], f32, kind="Internal").ap()
        O_SCR = nc.dram_tensor("scr_out", [BATCH, HEADS, VCOLS, TOKENS], f32, kind="Internal").ap()

        a_full, a_evac = sem("ring_a_filled"), sem("ring_a_evacuated")
        b_full, b_evac = sem("ring_b_filled"), sem("ring_b_evacuated")
        c_evac = sem("ring_c_evacuated")
        pv_done = sem("products_with_v")
        consts_in, x_in, modw_in, mask_in = sem("consts_in"), sem("x_in"), sem("mod_weights_in"), sem("masks_in")
        cond_ready, mod_ready, setup_dve = sem("cond_silu"), sem("mod_cols_ready"), sem("dve_setup_done")
        k_ones, mask_ready = sem("k_ones_ready"), sem("mask_bias_ready")
        w_in = {n: sem("in_" + n) for n in ("qkv", "o", "cq", "ckv", "w1", "w2", "gate", "rows", "misc", "rope3")}
        stats_ready, rstd_ready, xn_ready, xn_used = sem("stats_ready"), sem("roots_ready"), sem("xn_ready"), sem("xn_used")
        split_done = sem("split_done")
        scr_in = {w: sem("scratch_written_" + w) for w in "qk"}
        kc_in = sem("context_keys_in")
        ring_in = [sem(f"ring_loaded_{i}") for i in range(RING)]
        max_split, mx_out = sem("max_parts_ready"), sem("max_parts_out")
        max_in = [sem(f"max_rows_in_{i}") for i in range(RING)]
        ost_out = [sem(f"out_stage_written_{i}") for i in range(2)]
        den_in, recip_done, recip_out = sem("denominators_in"), sem("reciprocals_done"), sem("reciprocals_out")
        od_in, norm_done, x_add = sem("dense_out_in"), sem("out_normalised"), sem("residual_added")
        tk_sel, tk_arg, tk_exp = sem("top_k_marked"), sem("top_k_arguments"), sem("top_k_exps")
        gate_ready = sem("gate_ready")
        dve_step, pool_step, act_step = sem("dve_step"), sem("pool_step"), sem("act_step")
        stored = sem("stored")

        def bcast(ap, n):
            return ap.unsqueeze(1).broadcast_to([ap.shape[0], n, ap.shape[-1]])

        def w1_view(l):
            n = 2 * HIDDEN if LAYERS[l]["act"] == "swiglu" else HIDDEN
            return WR[:, 0:KF * n].rearrange("p (k f) -> p k f", k=KF)

        def mod_col(l, i, s, kf):
            return (NORMS.index((l, i)) * 2 + s) * KF + kf

        rope_of = {0: ROPE_L0, 3: ROPE_L3}

        def rope_cols(s, c):
            t = rope_of[s.l][:, c, :]
            if s.which == "ck":
                return bcast(t[:, 0:CTX], BATCH)
            at = (s.blk * BLOCK) % s.rope
            return t[:, at:at + BLOCK]

        def tok_view(ap, s):
            return ap[:, 0:s.width].rearrange("p (b t) -> p b t", b=BATCH) if s.which == "ck" else ap[:, 0:s.width]

        def keys_of(g):
            return CTX if g.cross else P

        block = ctx.enter_context(nc.Block())

        @block.sync
        def _(sp):
            def weight(name, dst, src):
                sp.dma_start(dst, src).then_inc(w_in[name], 16)

            def kp(w):
                return w.rearrange("(k p) f -> p k f", p=P)

            def row(v):
                return v.rearrange("(o f) -> o f", o=1).broadcast_to([P, v.shape[0]])

            for dst, src in ((IDF[:], ins["ident"]), (ROTM[:], ins["rotm"]),
                             (COND[:, 0], ins["cond"]), (MODB[:], ins["modb"]), (COLS[:], ins["cols"]),
                             (CTXT[:], ins["ctxt"]), (MISC[:], ins["rope0"])):
                sp.dma_start(dst, src).then_inc(consts_in, 16)
            for b in range(BATCH):
                sp.dma_start(X[:, b * TILES:(b + 1) * TILES, :],
                             ins["x"][b].rearrange("(t p) f -> p t f", p=P)).then_inc(x_in, 16)
            MODW = RINGS[:, :, :].rearrange("p a t -> p (a t)")[:, 0:KF * NCOLS // KF * FEAT]\
                .rearrange("p (k e f) -> p k e f", k=KF, e=NCOLS // KF)
            for e, (l, i) in enumerate(NORMS):
                for s in range(2):
                    src = ins[f"mod_{l}_{i}"][:, s * FEAT:(s + 1) * FEAT] if l == 3 else \
                        ins[f"mod_{l}"][:, LAYERS[l]["norms"][i][s] * FEAT:(LAYERS[l]["norms"][i][s] + 1) * FEAT]
                    sp.dma_start(MODW[:, :, e * 2 + s, :], kp(src)).then_inc(modw_in, 16)
            raw = PT[:, :, :, :].rearrange("p s h t -> p (s h t)")
            sp.dma_start(raw[:, 0:2048].bitcast(u8).rearrange("p (t q) -> p t q", t=TILES),
                         ins["mask_t"].rearrange("(t p) q -> p t q", p=P)).then_inc(mask_in, 16)
            sp.dma_start(raw[:, 2048:4096].bitcast(u8).rearrange("p (t q) -> p t q", t=TILES),
                         ins["mask_q"].rearrange("(t p) q -> p t q", p=P)).then_inc(mask_in, 16)
            sp.dma_start(JUNK[0:1, 0:BATCH * CTX // 2].bitcast(u8), ins["kv_row"]).then_inc(mask_in, 16)
            sp.dma_start(JUNK[0:CTX, 512:512 + BATCH // 2].bitcast(u8), ins["kv_col"]).then_inc(mask_in, 16)
            weight("qkv", WQKV[:], kp(ins["qkv_0"]))
            weight("o", WO[:], kp(ins["o_0"]))
            weight("cq", WCQ[:], kp(ins["cq_0"]))
            weight("ckv", WCKV[:], kp(ins["ckv_0"]))

            od = 0
            for s in steps:
                if s.kind == "gate":
                    if s.xadd:
                        sp.wait_ge(x_add, s.xadd)
                    l, i = s.l, s.i
                    if s.an is not None:
                        c = LAYERS[l]["gates"][i]
                        weight("gate", GW, kp(ins[f"mod_{l}"][:, c * FEAT:(c + 1) * FEAT]))
                    for j, name in enumerate((f"gb_{l}_{i}", f"ob_{l}_{i}", f"vb_{l}_{i}")):
                        weight("rows", BB[:, j, :], row(ins[name]))
                    if i == 1:
                        weight("o", WO[:], kp(ins[f"co_{l}"]))
                        weight("w1", w1_view(l), kp(ins[f"w1_{l}"]))
                        weight("w2", W2, kp(ins[f"w2_{l}"]))
                        if l + 1 < len(LAYERS):
                            weight("qkv", WQKV[:], kp(ins[f"qkv_{l + 1}"]))
                    if i == 2 and l + 1 < len(LAYERS):
                        weight("o", WO[:], kp(ins[f"o_{l + 1}"]))
                        weight("cq", WCQ[:], kp(ins[f"cq_{l + 1}"]))
                        weight("ckv", WCKV[:], kp(ins[f"ckv_{l + 1}"]))
                        if l == 0:
                            weight("misc", CTOK, ins["ctx"].rearrange("b t f -> t b f"))
                        if l == 2:
                            weight("rope3", WR[:, 6144:8192], ins["rope3"])
                elif s.kind == "scratch":
                    s = s.of
                    sp.wait_ge(split_done, s.split + 1)
                    for j, part in enumerate(PART_OF[s.which]):
                        sp.dma_start(QK_SCR[s.which][s.b, s.hh * 8:s.hh * 8 + 8, j], SPLIT[s.which][:, part, :])\
                            .then_inc(scr_in[s.which], 16)
                elif s.kind == "ctx_scratch":
                    s = s.of
                    sp.wait_ge(split_done, s.split + 1)
                    for j, part in enumerate(PART_OF["k"]):
                        sp.dma_start(KC_SCR[s.hh * 8:s.hh * 8 + 8, j], SPLIT["k"][:, part, 0:BATCH * CTX])\
                            .then_inc(scr_in["k"], 16)
                elif s.kind == "ctx_load":
                    sp.wait_ge(scr_in["k"], 96 * s.written)
                    sp.wait_ge(pv_done, s.pv)
                    for b in range(BATCH):
                        sp.dma_start(KC[0:PARTS, b, :, 0:CTX],
                                     KC_SCR[:, :, :, b * CTX:(b + 1) * CTX].rearrange("h j d t -> (j d) h t"))\
                            .then_inc(kc_in, 16)
                elif s.kind == "load":
                    g = s.g
                    if g.before is not None:
                        sp.wait_ge(pv_done, g.before.pv_last + 1)
                    for w, ring in (("q", Q6), ("k", K6)):
                        if w in g.written:
                            sp.wait_ge(scr_in[w], 96 * g.written[w])
                            sp.dma_start(ring[0:PARTS, g.slot], QK_SCR[w][g.b, g.g * GROUP:(g.g + 1) * GROUP]
                                         .rearrange("h j d t -> (j d) h t")).then_inc(ring_in[g.slot], 16)
                elif s.kind == "out_stage":
                    s = s.of
                    sp.wait_ge(c_evac, s.cn + 1)
                    sp.dma_start(O_SCR[s.g.b, s.g.g * GROUP:(s.g.g + 1) * GROUP, :, s.qh * BLOCK:(s.qh + 1) * BLOCK],
                                 OST[:, s.ost % 2, :]).then_inc(ost_out[s.ost % 2], 16)
                elif s.kind == "dense":
                    sp.wait_ge(ost_out[0], 16 * ((s.ost + 2) // 2))
                    if s.ost >= 1:
                        sp.wait_ge(ost_out[1], 16 * ((s.ost + 1) // 2))
                    if s.n:
                        sp.wait_ge(norm_done, s.n)
                    sp.dma_start(DEN[:, 0:TOKENS // HEAD], O_SCR[s.b, s.hh * 8:s.hh * 8 + 8, HEAD]
                                 .rearrange("h (c t) -> h c t", c=HEAD)).then_inc(den_in, 16)
                    cuts = [(0, TOKENS, 0)]
                    if s.akind == "window":
                        cuts = [(SHIFT, TOKENS, 0), (0, SHIFT, TOKENS - SHIFT)]
                    for lo, hi, at in cuts:
                        sp.dma_start(HT[:, s.hh, s.b, lo:hi], O_SCR[s.b, s.hh * 8:s.hh * 8 + 8, 0:HEAD, at:at + hi - lo])\
                            .then_inc(od_in, 16)
                        od += 16
                elif s.kind == "reciprocal":
                    s = s.of
                    sp.wait_ge(recip_done, s.n + 1)
                    sp.dma_start(R_SCR[s.n % 2].rearrange("h (c t) -> h c t", c=HEAD), DEN[:, 0:TOKENS // HEAD])\
                        .then_inc(recip_out, 16)
                    sp.wait_ge(recip_out, 16 * (s.n + 1))
                    cuts = [(0, TOKENS, 0)]
                    if s.akind == "window":
                        cuts = [(SHIFT, TOKENS, 0), (0, SHIFT, TOKENS - SHIFT)]
                    for lo, hi, at in cuts:
                        sp.dma_start(DEN[:, lo:hi], R_SCR[s.n % 2, :, at:at + hi - lo].unsqueeze(1)
                                     .broadcast_to([8, HEAD, hi - lo])).then_inc(od_in, 16)
                        od += 16
                    s.need = od
                elif s.kind == "store":
                    sp.wait_ge(x_add, s.xadd)
                    t = BLOCK // P
                    sp.dma_start(out[s.b, s.blk * BLOCK:(s.blk + 1) * BLOCK].rearrange("(t p) f -> p t f", p=P),
                                 X[:, s.b * TILES + s.blk * t:s.b * TILES + (s.blk + 1) * t, :]).then_inc(stored, 16)
            sp.wait_ge(stored, 16 * BATCH * BLOCKS)

        @block.tensor
        def _(pe):
            def need_a(n):
                if n >= A_SLOTS:
                    pe.wait_ge(a_evac, n - A_SLOTS + 1)
                return PA[:, n % A_SLOTS, :]

            def need_b(n):
                if n >= B_SLOTS:
                    pe.wait_ge(b_evac, n - B_SLOTS + 1)
                return PB[:, n % B_SLOTS, :]

            mm = nc.tensor.matmul
            MODW = RINGS[:, :, :].rearrange("p a t -> p (a t)")[:, 0:KF * NCOLS // KF * FEAT]\
                .rearrange("p (k e f) -> p k e f", k=KF, e=NCOLS // KF)
            pe.wait_ge(cond_ready, 1)
            pe.wait_ge(modw_in, 16 * 2 * len(NORMS))
            ps = PA[:, 0, :].rearrange("p (c b) -> p c b", b=BATCH)
            for e, (l, i) in enumerate(NORMS):
                for s in range(2):
                    for m in range(KF):
                        c = (e * 2 + s) * KF + m
                        for k in range(KF):
                            last = mm(ps[:, c, :], MODW[:, k, e * 2 + s, m * P:(m + 1) * P],
                                      COND[:, int(LAYERS[l]["silu_cond"]), k, :], start=k == 0, stop=k == KF - 1)
            last.then_inc(a_full, 1)
            n_o = n_gate = 0
            for s in steps:
                if s.kind == "norm":
                    pe.wait_ge(xn_ready, s.xn + 1)
                    for kf in range(KF):
                        ps = need_b(s.b0 + kf)
                        for t in range(BLOCK // P):
                            last = nc.tensor.transpose(ps[:, t * P:(t + 1) * P],
                                                       XN[:, s.xn % 2, t, kf * P:(kf + 1) * P], IDF[:])
                        last.then_inc(b_full, 1)
                elif s.kind == "gate" and s.an is not None:
                    n_gate += 1
                    pe.wait_ge(w_in["gate"], 16 * n_gate)
                    ps = need_a(s.an)
                    for b in range(BATCH):
                        for k in range(KF):
                            c = COND[:, int(LAYERS[s.l]["silu_cond"]), k, b:b + 1].broadcast_to([P, P])
                            last = mm(ps[:, b * FEAT:(b + 1) * FEAT], c, GW[:, k, :], start=k == 0, stop=k == KF - 1)
                    last.then_inc(a_full, 1)
                elif s.kind == "context_norm" and s.b0 is not None:
                    pe.wait_ge(xn_ready, s.xn + 1)
                    for kf in range(KF):
                        ps = need_b(s.b0 + kf)
                        for b in range(BATCH):
                            last = nc.tensor.transpose(ps[:, b * CTX:(b + 1) * CTX],
                                                       CNRM[:, b, kf * P:(kf + 1) * P], IDF[0:CTX, 0:CTX])
                        last.then_inc(b_full, 1)
                elif s.kind == "project":
                    if s.which == "ck":
                        pe.wait_ge(w_in["ckv"], 16 * (s.l + 1))
                        w, at = WCKV, 0
                        src = CTN if s.l == 1 else CTXT
                        if s.l == 1:
                            pe.wait_ge(b_evac, s.bn - s.hh)
                    else:
                        pe.wait_ge(b_evac, s.ht + 1)
                        if s.cross:
                            pe.wait_ge(w_in["cq"], 16 * (s.l + 1))
                            w, at = WCQ, 0
                        else:
                            pe.wait_ge(w_in["qkv"], 16 * (s.l + 1))
                            w, at = WQKV, FEAT * (s.which == "k")
                        src = HT[:, :, s.b, s.blk * BLOCK:(s.blk + 1) * BLOCK]
                    ps = need_b(s.bn)
                    for k in range(KF):
                        last = mm(ps[:, 0:s.width], w[:, k, at + s.hh * P:at + (s.hh + 1) * P], src[:, k, 0:s.width],
                                  start=k == 0, stop=k == KF - 1)
                    last.then_inc(b_full, 1)
                elif s.kind == "rotate":
                    s = s.of
                    pe.wait_ge(b_evac, s.bn + 1)
                    mm(need_a(s.an)[:, 0:s.width], ROTM[:], RAW[:, s.split % 2, 0:s.width],
                       start=True, stop=True).then_inc(a_full, 1)
                elif s.kind == "v":
                    pe.wait_ge(b_evac, s.ht + 1)
                    ps = need_a(s.an)
                    for t in range(4):
                        tok = (s.u * 4 + t) * P
                        for k in range(KF):
                            last = mm(ps[:, t * FEAT:(t + 1) * FEAT], HT[:, k, s.b, tok:tok + P],
                                      WQKV[:, k, 2 * FEAT:3 * FEAT], start=k == 0, stop=k == KF - 1)
                    last.then_inc(a_full, 1)
                elif s.kind == "ctx_v":
                    ps = need_a(s.an)
                    src = CTN if s.l == 1 else CTXT
                    for k in range(KF):
                        last = mm(ps[0:CTX, 0:FEAT], src[:, k, s.b * CTX:(s.b + 1) * CTX],
                                  WCKV[:, k, FEAT:2 * FEAT], start=k == 0, stop=k == KF - 1)
                    last.then_inc(a_full, 1)
                elif s.kind in ("first", "topk"):
                    g = s.g
                    pe.wait_ge(ring_in[g.slot], 16 * g.filled)
                    if g.cross:
                        pe.wait_ge(kc_in, 32 * (g.l + 1))
                    ps = need_a(s.an)
                    if g.akind == "full":
                        h, t = s.u // TILES, s.u % TILES
                        for half in range(2):
                            last = mm(ps[:, half * BLOCK:(half + 1) * BLOCK], Q6[0:PARTS, g.slot, h, t * P:(t + 1) * P],
                                      K6[0:PARTS, g.slot, h, half * BLOCK:(half + 1) * BLOCK], start=True, stop=True)
                    elif g.akind == "window":
                        for i in range(8):
                            h, w = 2 * s.t + i // 4, s.qh * BLOCK + i % 4 * P
                            last = mm(ps[:, i * P:(i + 1) * P], Q6[0:PARTS, g.slot, h, w:w + P],
                                      K6[0:PARTS, g.slot, h, w:w + P], start=True, stop=True)
                    else:
                        pair = s.qh * 2 + s.t
                        if g.l == 0:
                            pe.wait_ge(mask_ready, 4)
                        for t in range(2):
                            for h in range(GROUP):
                                at = t * BLOCK + h * P
                                tok = (pair * 2 + t) * P
                                masked = LAYERS[g.l]["mask"]
                                if masked:
                                    mm(ps[:, at:at + CTX], ONE[0:1, :], MROW[0:1, g.b, :], start=True, stop=False)
                                last = mm(ps[:, at:at + CTX], Q6[0:PARTS, g.slot, h, tok:tok + P],
                                          KC[0:PARTS, g.b, g.g * GROUP + h, 0:CTX], start=not masked, stop=True)
                    last.then_inc(a_full, 1)
                elif s.kind == "max":
                    pe.wait_ge(a_evac, s.g.last_a + 1)
                    nc.tensor.transpose(need_b(s.g.max_b)[0:GROUP * TILES, 0:P], NM[:, s.m % 2, :], IDF[:])\
                        .then_inc(b_full, 1)
                elif s.kind == "scores":
                    s, h0, bn = s.of, s.h0, s.bn
                    g = s.g
                    pe.wait_ge(max_in[g.slot], 16 * g.max_filled)
                    pe.wait_ge(k_ones, g.l + 1)
                    if LAYERS[g.l]["mask"]:
                        pe.wait_ge(mask_ready, 4)
                    q0 = s.qh * BLOCK
                    for h in (h0, h0 + 1):
                        ps = need_b(bn + h - h0)
                        masked = LAYERS[g.l]["mask"]
                        if masked:
                            mm(ps[:, :], IDB[:], MASKT[:, s.kt, q0:q0 + BLOCK], start=True, stop=False)
                        last = mm(ps[:, :], K6[0:ROWS, g.slot, h, s.kt * P:(s.kt + 1) * P],
                                  Q6[0:ROWS, g.slot, h, q0:q0 + BLOCK], start=not masked, stop=True)
                        last.then_inc(b_full, 1)
                elif s.kind == "topk_turn":
                    k = s.of
                    pe.wait_ge(tk_exp, k.n + 1)
                    for t in range(2):
                        ps = need_b(k.bn + t)
                        for i in range(4):
                            if k.g.akind == "window":
                                last = nc.tensor.transpose(ps[:, i * P:(i + 1) * P],
                                                           EW[:, k.n % 3, (t * 4 + i) * P:(t * 4 + i + 1) * P], IDF[:])
                            else:
                                e = EP[k.sel % 2] if k.g.select else EX[:, k.n % 3]
                                last = nc.tensor.transpose(ps[0:CTX, i * P:(i + 1) * P], e[:, t * GROUP + i, :], IDF[:])
                        last.then_inc(b_full, 1)
                elif s.kind == "pv":
                    s = s.of
                    g, n = s.g, keys_of(s.g)
                    pe.wait_ge(b_evac, s.last_b + 1)
                    pe.wait_ge(a_evac, s.v_a + 1)
                    if s.kt == 0 and s.cn:
                        pe.wait_ge(c_evac, s.cn)
                    for h in range(GROUP):
                        o = PC[VCOLS * h:VCOLS * (h + 1), :]
                        head = g.g * GROUP + h
                        if g.akind == "window":
                            for i in range(BLOCK // WINDOW):
                                last = mm(o[:, i * P:(i + 1) * P], VA[:, s.qh * 4 + i, head, :],
                                          PT[:, s.pv % 2, h, i * P:(i + 1) * P], start=True, stop=True)
                        else:
                            last = mm(o, VA[0:n, g.b if g.cross else s.kt, head, :], PT[0:n, s.pv % 2, h, :],
                                      start=s.kt == 0, stop=s.last)
                    last.then_inc(pv_done, 1)
                elif s.kind == "out":
                    pe.wait_ge(norm_done, s.od)
                    pe.wait_ge(w_in["o"], 16 * (2 * s.l + int(s.cross) + 1))
                    ps = need_a(s.an)
                    for t in range(2):
                        tok = (s.u * 2 + t) * P
                        for k in range(KF):
                            last = mm(ps[:, t * FEAT:(t + 1) * FEAT], HT[:, k, s.b, tok:tok + P], WO[:, k, :],
                                      start=k == 0, stop=k == KF - 1)
                    last.then_inc(a_full, 1)
                elif s.kind == "up":
                    pe.wait_ge(b_evac, s.ht + 1)
                    pe.wait_ge(w_in["w1"], 16 * (s.l + 1))
                    w1 = w1_view(s.l)
                    for ps, at, full in ((need_b(s.bn), 0, b_full),) + (
                            ((need_a(s.an), HIDDEN, a_full),) if s.an is not None else ()):
                        for k in range(KF):
                            last = mm(ps[:, 0:BLOCK], w1[:, k, at + s.j * P:at + (s.j + 1) * P],
                                      HT[:, k, s.b, s.blk * BLOCK:(s.blk + 1) * BLOCK], start=k == 0, stop=k == KF - 1)
                        last.then_inc(full, 1)
                elif s.kind == "down":
                    pe.wait_ge(w_in["w2"], 16 * (s.l + 1))
                    pe.wait_ge(b_evac, s.hid_b)
                    if LAYERS[s.l]["act"] == "swiglu":
                        pe.wait_ge(a_evac, s.hid_a)
                    ps = need_a(s.an)
                    for t in range(2):
                        tok = (s.u * 2 + t) * P
                        for k in range(HIDDEN // P):
                            last = mm(ps[:, t * FEAT:(t + 1) * FEAT], HID[s.par][:, k, tok:tok + P], W2[:, k, :],
                                      start=k == 0, stop=k == HIDDEN // P - 1)
                    last.then_inc(a_full, 1)

        @block.scalar
        def _(act):
            def from_b(n):
                act.wait_ge(b_full, n + 1)
                return PB[:, n % B_SLOTS, :]

            f = nc.scalar.activation
            act.wait_ge(consts_in, 16 * 7)
            f(COND[:, 1], COND[:, 0], ACT.Silu).then_inc(cond_ready, 1)
            act.wait_ge(mod_ready, 1)
            for s in steps:
                if s.kind == "stats":
                    act.wait_ge(stats_ready, s.stats + 1)
                    f(RSTD[:, s.b, :], MV[:, s.b, :, 1], ACT.Sqrt).then_inc(rstd_ready, 1)
                elif s.kind == "norm":
                    for kf in range(KF):
                        ps = from_b(s.b0 + kf)
                        has = (s.l, s.i) in NORMS
                        kw = dict(scale=MODC[:, mod_col(s.l, s.i, 0, kf), s.b:s.b + 1],
                                  bias=MODC[:, mod_col(s.l, s.i, 1, kf), s.b:s.b + 1]) if has else {}
                        lo = s.blk * BLOCK
                        cuts = [(0, BLOCK, lo)]
                        if s.i == 0 and LAYERS[s.l]["kind"] == "window":
                            cuts = [(0, SHIFT, TOKENS - SHIFT), (SHIFT, BLOCK, 0)] if s.blk == 0 else \
                                [(0, BLOCK, lo - SHIFT)]
                        for a, z, at in cuts:
                            last = f(HT[:, kf, s.b, at:at + z - a], ps[:, a:z], ACT.Identity, **kw)
                        last.then_inc(b_evac, 1)
                elif s.kind == "context_norm" and s.b0 is not None:
                    act.wait_ge(stats_ready, s.stats + 1)
                    f(RSTD[0:CTX, 0, 0:BATCH], MV[0:CTX, 0, 0:BATCH, 1], ACT.Sqrt).then_inc(rstd_ready, 1)
                    for kf in range(KF):
                        f(CTN[:, kf, :], from_b(s.b0 + kf)[:, 0:BATCH * CTX], ACT.Copy).then_inc(b_evac, 1)
                elif s.kind == "project":
                    ps = from_b(s.bn)
                    if s.split >= 2:
                        act.wait_ge(split_done, s.split - 1)
                    col = {"q": 4 if s.cross else 0, "k": 2, "ck": 6}[s.which] + s.hh
                    f(RAW[:, s.split % 2, 0:s.width], ps[:, 0:s.width], ACT.Identity,
                      bias=COLS[:, s.l, col:col + 1], scale=0.25 if s.which == "q" else 1.0).then_inc(
                        act_step if not s.rope else b_evac, 1)
                    if not s.rope:
                        buf = s.which[-1]
                        if s.before:
                            act.wait_ge(scr_in[buf], 96 * s.before)
                        f(SPLIT[buf][:, 0, s.blk * BLOCK:s.blk * BLOCK + s.width], ps[:, 0:s.width], ACT.Identity,
                          bias=COLS[:, s.l, col:col + 1], scale=0.25 if s.which == "q" else 1.0).then_inc(b_evac, 1)
                elif s.kind == "max":
                    ps = from_b(s.g.max_b)
                    if s.m >= 2:
                        act.wait_ge(max_split, s.m - 1)
                    f(NT[:, s.m % 2, :], ps[0:GROUP * TILES, 0:P], ACT.Copy, scale=-1.0).then_inc(b_evac, 1)
                elif s.kind == "scores":
                    s, h0, bn = s.of, s.h0, s.bn
                    n = keys_of(s.g)
                    for h in (h0, h0 + 1):
                        ps = from_b(bn + h - h0)
                        if s.pv >= 2:
                            act.wait_ge(pv_done, s.pv - 1)
                        f(PT[0:n, s.pv % 2, h, :], ps[0:n, :], ACT.Exp).then_inc(b_evac, 1)
                elif s.kind == "topk_turn":
                    k = s.of
                    if k.g.select:
                        act.wait_ge(tk_arg, k.sel + 1)
                    else:
                        act.wait_ge(a_evac, k.an + 1)
                    e = EW[:, k.n % 3] if k.g.akind == "window" else EP[k.sel % 2] if k.g.select else EX[:, k.n % 3]
                    f(e, e, ACT.Exp).then_inc(tk_exp, 1)
                    if k.of.pv >= 2:
                        act.wait_ge(pv_done, k.of.pv - 1)
                    for t in range(2):
                        ps = from_b(k.bn + t)
                        if k.g.akind == "window":
                            f(PT[:, k.of.pv % 2, 2 * k.t + t, :], ps, ACT.Copy).then_inc(b_evac, 1)
                        else:
                            at = (k.t * 2 + t) * P
                            f(PT[0:CTX, k.of.pv % 2, :, at:at + P], ps[0:CTX, :].rearrange("p (h t) -> p h t", h=GROUP),
                              ACT.Copy).then_inc(b_evac, 1)
                elif s.kind == "out_stage":
                    s = s.of
                    act.wait_ge(pv_done, s.pv + 1)
                    if s.ost >= 2:
                        act.wait_ge(ost_out[s.ost % 2], 16 * (s.ost // 2))
                    f(OST[:, s.ost % 2, :], PC[:, :], ACT.Copy).then_inc(c_evac, 1)
                elif s.kind == "up":
                    ps = from_b(s.bn)
                    fn = {"tanh": ACT.Gelu_apprx_tanh, "erf": ACT.Gelu, "swiglu": ACT.Silu}[LAYERS[s.l]["act"]]
                    f(HID[s.par][:, s.j, :], ps, fn, bias=COLS[:, s.l, 8 + s.j:9 + s.j]).then_inc(b_evac, 1)

        @block.vector
        def _(dve):
            chain = [0]

            def link(ins_):
                chain[0] += 1
                ins_.then_inc(dve_step, 1)
                dve.wait_ge(dve_step, chain[0])

            def from_a(n):
                dve.wait_ge(a_full, n + 1)
                return PA[:, n % A_SLOTS, :]

            v = nc.vector

            def variance(var, eps):
                v.tensor_scalar(var, var, eps, None, ALU.add).then_inc(stats_ready, 1)

            def rstd(y, var, t, n):
                dve.wait_ge(rstd_ready, n + 1)
                link(v.reciprocal(y, y))
                link(v.tensor_tensor(t, y, y, ALU.mult))
                link(v.tensor_tensor(t, t, var, ALU.mult))
                link(v.tensor_scalar(t, t, -0.5, 1.5, ALU.mult, ALU.add))
                link(v.tensor_tensor(y, y, t, ALU.mult))

            v.memset(VA[:], 1.0).then_inc(setup_dve, 1)
            v.memset(ONE, 1.0).then_inc(setup_dve, 1)
            dve.wait_ge(consts_in, 16 * 7)
            link(v.tensor_copy(IDB[:], IDF[:]))
            link(v.tensor_scalar(COLS[:, :, 0:2], COLS[:, :, 0:2], 0.25, None, ALU.mult))
            link(v.tensor_scalar(COLS[:, :, 4:6], COLS[:, :, 4:6], 0.25, None, ALU.mult))
            dve.wait_ge(a_full, 1)
            ps = PA[:, 0, 0:NCOLS * BATCH].rearrange("p (c b) -> p c b", b=BATCH)
            for b in range(BATCH):
                last = v.tensor_tensor(MODC[:, :, b], ps[:, :, b], MODB[:, 0, :], ALU.add)
            last.then_inc(a_evac, 1)
            dve.wait_ge(a_evac, 1)
            for b in range(BATCH):
                m = MODC[:, :, b].rearrange("p (e s k) -> p e s k", s=2, k=KF)[:, :, 0, :]
                w = MODB[:, 1, :].rearrange("p (e s k) -> p e s k", s=2, k=KF)[:, :, 0, :]
                last = v.scalar_tensor_tensor(out=m, in0=m, scalar=1.0, in1=w, op0=ALU.add, op1=ALU.mult)
            last.then_inc(mod_ready, 1)
            dve.wait_ge(mask_ready, 4)
            n_rows = 0
            for s in steps:
                if s.kind == "stats":
                    dve.wait_ge(x_in, 32)
                    if s.xadd:
                        dve.wait_ge(x_add, s.xadd)
                    for t in range(TILES):
                        last = v.bn_stats(STAT[:, t, :], X[:, s.b * TILES + t, :])
                    link(last)
                    for t in range(TILES):
                        last = v.bn_aggr(MV[:, s.b, t, :], STAT[:, t, :])
                    link(last)
                    variance(MV[:, s.b, :, 1], LAYERS[s.l]["eps"])
                    rstd(RSTD[:, s.b, :], MV[:, s.b, :, 1], STAT[:, :, 0], s.stats)
                elif s.kind == "norm":
                    if s.xn >= 2:
                        dve.wait_ge(b_full, s.xn_b)
                    for t in range(4):
                        tile = s.blk * 4 + t
                        last = v.tensor_scalar(XN[:, s.xn % 2, t, :], X[:, s.b * TILES + tile, :],
                                               MV[:, s.b, tile, 0:1], RSTD[:, s.b, tile:tile + 1],
                                               ALU.subtract, ALU.mult)
                    last.then_inc(xn_ready, 1)
                elif s.kind == "context_norm" and s.b0 is not None:
                    dve.wait_ge(w_in["misc"], 16)
                    for b in range(BATCH):
                        last = v.bn_stats(STAT[0:CTX, b, :], CTOK[:, b, :])
                    link(last)
                    for b in range(BATCH):
                        last = v.bn_aggr(MV[0:CTX, 0, b, :], STAT[0:CTX, b, :])
                    link(last)
                    variance(MV[0:CTX, 0, 0:BATCH, 1], LAYERS[s.l]["eps"])
                    rstd(RSTD[0:CTX, 0, 0:BATCH], MV[0:CTX, 0, 0:BATCH, 1], STAT[0:CTX, 0:BATCH, 0], s.stats)
                    for b in range(BATCH):
                        last = v.tensor_scalar(CNRM[:, b, :], CTOK[:, b, :], MV[0:CTX, 0, b, 0:1],
                                               RSTD[0:CTX, 0, b:b + 1], ALU.subtract, ALU.mult)
                    last.then_inc(xn_ready, 1)
                elif s.kind == "gate":
                    n_rows += 3
                    dve.wait_ge(w_in["rows"], 16 * n_rows)
                    if s.an is not None:
                        ps = from_a(s.an)[:, 0:BATCH * FEAT].rearrange("p (b f) -> p b f", b=BATCH)
                        v.tensor_tensor(GB[:, :, 0, :], ps, bcast(BB[:, 0, :], BATCH), ALU.add).then_inc(a_evac, 1)
                        dve.wait_ge(a_evac, s.an + 1)
                        v.tensor_tensor(GB[:, :, 1, :], GB[:, :, 0, :], bcast(BB[:, 1, :], BATCH), ALU.mult)\
                            .then_inc(gate_ready, 1)
                elif s.kind == "split":
                    s = s.of
                    buf = s.which[-1]
                    r = RAW[:, s.split % 2, 0:s.width]
                    parts = SPLIT[buf][:, :, s.blk * BLOCK:s.blk * BLOCK + s.width]
                    dve.wait_ge(b_evac, s.bn + 1)
                    if s.before:
                        dve.wait_ge(scr_in[buf], 96 * s.before)
                    if s.rope:
                        if s.l == 3:
                            dve.wait_ge(w_in["rope3"], 16)
                        ps = from_a(s.an)
                        v.tensor_tensor(tok_view(ROT, s), tok_view(ps, s), rope_cols(s, 1), ALU.mult).then_inc(a_evac, 1)
                        rv = tok_view(RAW[:, s.split % 2, :], s)
                        link(v.tensor_tensor(rv, rv, rope_cols(s, 0), ALU.mult))
                        dve.wait_ge(a_evac, s.an + 1)
                        link(v.tensor_tensor(r, r, ROT[:, 0:s.width], ALU.add))
                        link(v.tensor_copy(parts[:, 0, :], r))
                    link(v.tensor_tensor(r, r, parts[:, 0, :], ALU.subtract))
                    link(v.tensor_copy(parts[:, 1, :], r))
                    v.tensor_tensor(parts[:, 2, :], r, parts[:, 1, :], ALU.subtract).then_inc(split_done, 1)
                elif s.kind in ("v", "ctx_v"):
                    ps = from_a(s.an)
                    i = int(s.kind == "ctx_v")
                    n = CTX if i else P
                    tiles = slice(s.b, s.b + 1) if i else slice(s.u * 4, s.u * 4 + 4)
                    nt = 1 if i else 4
                    dst = VA[0:n, tiles, :, 0:HEAD]
                    src = ps[0:n, 0:nt * FEAT].rearrange("p (t h d) -> p t h d", t=nt, h=HEADS)
                    for t in range(nt):
                        bias = BB[0:n, 2, :].rearrange("p (h d) -> p h d", h=HEADS)
                        last = v.tensor_tensor(dst[:, t], src[:, t], bias, ALU.add)
                    last.then_inc(a_evac, 1)
                elif s.kind == "first":
                    g = s.g
                    ps = from_a(s.an)
                    if g.akind == "full" and LAYERS[g.l]["mask"]:
                        dve.wait_ge(mask_ready, 4)
                        h, t = s.u // TILES, s.u % TILES
                        dve.wait_ge(a_evac, s.an)
                        v.tensor_tensor_reduce(out=JUNK[:], in0=ps, in1=MASKQ[:, t, :], scale=1.0, scalar=-3.4e38,
                                               op0=ALU.add, op1=ALU.max, accum_out=NM[:, g.m % 2, s.u:s.u + 1])\
                            .then_inc(a_evac, 1)
                    else:
                        v.tensor_reduce(NM[:, g.m % 2, s.u:s.u + 1], ps, AX.X, ALU.max).then_inc(a_evac, 1)
                elif s.kind == "topk" and not s.g.select:
                    p2 = s.n % 2
                    n = P if s.g.akind == "window" else CTX
                    ps = from_a(s.an).rearrange("p (q h k) -> p q h k", q=2, k=P)[:, :, 0:GROUP, 0:n]
                    e = (EW[:, s.n % 3].rearrange("p (i k) -> p i k", k=P) if n == P else EX[:, s.n % 3])
                    for t in range(2):
                        last = v.tensor_reduce(NM[:, p2, t * 4:t * 4 + 4], ps[:, t], AX.X, ALU.max)
                    link(last)
                    if s.reuse is not None:
                        dve.wait_ge(b_full, s.reuse.bn + 2)
                    for t in range(2):
                        m = NM[:, p2, t * 4:t * 4 + 4].unsqueeze(2).broadcast_to([P, 4, n])
                        last = v.tensor_tensor(e[:, t * 4:t * 4 + 4, :], ps[:, t], m, ALU.subtract)
                    last.then_inc(a_evac, 1)
                elif s.kind == "topk":
                    p2 = s.sel % 2
                    ps = from_a(s.an).rearrange("p (q h k) -> p q h k", q=2, k=P)
                    if s.sel >= 2:
                        dve.wait_ge(tk_arg, s.sel - 1)
                    for t in range(2):
                        last = v.tensor_copy(TS[:, p2, t * GROUP:(t + 1) * GROUP, :], ps[:, t, 0:GROUP, 0:CTX])
                    last.then_inc(a_evac, 1)
                    dve.wait_ge(a_evac, s.an + 1)
                    for i in range(8):
                        last = v.max(M8[:, p2, i, :], TS[:, p2, i, :])
                    link(last)
                    for i in range(8):
                        last = v.match_replace(S3[:, p2, i, :], M8[:, p2, i, :], TS[:, p2, i, :], GONE)
                    link(last)
                    for i in range(8):
                        last = v.max(M8B[:, i, :], S3[:, p2, i, :])
                    link(last)
                    for i in range(8):
                        last = v.match_replace(S3[:, p2, i, :], M8B[:, i, :], S3[:, p2, i, :], GONE)
                    last.then_inc(tk_sel, 1)
                    dve.wait_ge(tk_sel, s.sel + 1)
                elif s.kind == "reciprocal":
                    s = s.of
                    dve.wait_ge(den_in, 16 * (s.n + 1))
                    v.reciprocal(DEN[:, 0:TOKENS // HEAD], DEN[:, 0:TOKENS // HEAD]).then_inc(recip_done, 1)
                elif s.kind == "normalise":
                    s = s.of
                    dve.wait_ge(od_in, s.need)
                    v.tensor_tensor(HT[:, s.hh, s.b, :], HT[:, s.hh, s.b, :], DEN[:], ALU.mult).then_inc(norm_done, 1)
                elif s.kind in ("out", "down"):
                    i = 2 if s.kind == "down" else int(s.cross)
                    ps = from_a(s.an)[:, 0:2 * FEAT].rearrange("p (t f) -> p t f", t=2)
                    if s.xadd:
                        dve.wait_ge(x_add, s.xadd)
                    if LAYERS[s.l]["gates"][i] is not None:
                        v.tensor_tensor(TMP[:], ps, bcast(GB[:, s.b, 0, :], 2), ALU.mult).then_inc(a_evac, 1)
                    else:
                        v.tensor_tensor(TMP[:], ps, bcast(BB[:, 1, :], 2), ALU.add).then_inc(a_evac, 1)
                elif s.kind == "up" and s.an is not None:
                    ps = from_a(s.an)
                    dve.wait_ge(b_evac, s.bn + 1)
                    v.scalar_tensor_tensor(out=HID[s.par][:, s.j, :], in0=ps[:, 0:BLOCK],
                                           scalar=COLS[:, s.l, 16 + s.j:17 + s.j], in1=HID[s.par][:, s.j, :],
                                           op0=ALU.add, op1=ALU.mult).then_inc(a_evac, 1)

        @block.gpsimd
        def _(pool):
            chain = [0]

            def link(ins_):
                chain[0] += 1
                ins_.then_inc(pool_step, 1)
                pool.wait_ge(pool_step, chain[0])

            g_ = nc.gpsimd
            pool.wait_ge(mask_in, 64)
            raw = PT[:, :, :, :].rearrange("p s h t -> p (s h t)")
            for n, (dst, src) in enumerate(((MASKT, raw[:, 0:2048].bitcast(u8).rearrange("p (t q) -> p t q", t=TILES)),
                             (MASKQ, raw[:, 2048:4096].bitcast(u8).rearrange("p (t q) -> p t q", t=TILES)),
                             (MROW.rearrange("p b t -> p (b t)"), JUNK[0:1, 0:BATCH * CTX // 2].bitcast(u8)),
                             (MCOL[:], JUNK[0:CTX, 512:512 + BATCH // 2].bitcast(u8)))):
                (g_.tensor_scalar(dst, src, -1.0, -NEG, ALU.add, ALU.mult)
                 .then_inc(mask_ready, 1))
                pool.wait_ge(mask_ready, n + 1)
            pool.wait_ge(a_evac, 1)
            g_.memset(K6[PARTS:P, :, :, :], 1.0).then_inc(k_ones, 1)
            pool.wait_ge(k_ones, 1)
            for s in steps:
                if s.kind == "gate":
                    if s.l < 3 and s.i == 2:
                        pool.wait_ge(x_add, s.xadd)
                        g_.memset(K6[PARTS:P, 2, :, :], 1.0).then_inc(k_ones, 1)
                        pool.wait_ge(k_ones, s.l + 2)
                elif s.kind == "max":
                    p2 = s.m % 2
                    pool.wait_ge(b_evac, s.g.max_b + 1)
                    r, parts = NT[:, p2, :], MS[:, p2]
                    link(g_.tensor_copy(parts[:, 0, :], r))
                    link(g_.tensor_tensor(out=r, in0=r, in1=parts[:, 0, :], op=ALU.subtract))
                    link(g_.tensor_copy(parts[:, 1, :], r))
                    g_.tensor_tensor(out=parts[:, 2, :], in0=r, in1=parts[:, 1, :], op=ALU.subtract)\
                        .then_inc(max_split, 1)
                    pool.wait_ge(max_split, s.m + 1)
                    pool.dma_start(MX_SCR[p2].rearrange("j r t -> r j t"), MS[:, p2]).then_inc(mx_out, 16)
                    pool.wait_ge(mx_out, 16 * (s.m + 1))
                    pool.dma_start(Q6[PARTS:ROWS, s.g.slot].rearrange("p h t -> p (h t)"),
                                   MX_SCR[p2].rearrange("j r t -> j (r t)")).then_inc(max_in[s.g.slot], 16)
                elif s.kind == "topk" and s.g.select:
                    p2 = s.sel % 2
                    pool.wait_ge(tk_sel, s.sel + 1)
                    link(g_.tensor_scalar(S3[:, p2], S3[:, p2], GONE * 0.9, -1.0e30, ALU.is_gt, ALU.mult))
                    if s.reuse is not None:
                        pool.wait_ge(b_full, s.reuse.bn + 2)
                    m = M8[:, p2, :, 0:1].broadcast_to([P, 8, CTX])
                    link(g_.tensor_tensor(out=EP[p2], in0=TS[:, p2], in1=m, op=ALU.subtract))
                    g_.tensor_tensor(out=EP[p2], in0=EP[p2], in1=S3[:, p2], op=ALU.add).then_inc(tk_arg, 1)
                    pool.wait_ge(tk_arg, s.sel + 1)
                elif s.kind in ("out", "down"):
                    i = 2 if s.kind == "down" else int(s.cross)
                    pool.wait_ge(a_evac, s.an + 1)
                    if LAYERS[s.l]["gates"][i] is not None:
                        pool.wait_ge(gate_ready, s.gate)
                        link(g_.tensor_tensor(out=TMP[:], in0=TMP[:], in1=bcast(GB[:, s.b, 1, :], 2), op=ALU.add))
                    t0 = s.b * TILES + (s.blk * 4 if s.kind == "down" else 0) + s.u * 2
                    g_.tensor_tensor(out=X[:, t0:t0 + 2, :], in0=X[:, t0:t0 + 2, :], in1=TMP[:], op=ALU.add)\
                        .then_inc(x_add, 1)
                    pool.wait_ge(x_add, s.xadd + 1)


def kernel(**inputs):
    import concourse.bacc as bacc
    from concourse.bass_utils import run_bass_kernel_spmd

    a = {k: np.asarray(v) for k, v in inputs.items()}
    zeros = np.zeros
    f32 = np.float32

    def cols(v):
        return v.reshape(-1, P).T

    def rope_table(n, repeat):
        inv = 1.0 / 10000.0 ** (np.arange(0, HEAD, 2, dtype=f32) / f32(HEAD))
        ang = np.outer(np.concatenate([inv, inv]), np.arange(n, dtype=f32)).astype(f32)
        sign = np.concatenate([-np.ones(HEAD // 2), np.ones(HEAD // 2)])[:, None]
        return np.stack([np.tile(np.cos(ang), (8, 1)), np.tile(np.sin(ang) * sign, (8, 1))], 1).astype(f32)

    rot = zeros((P, P), f32)
    for o in range(P):
        rot[(o // HEAD) * HEAD + (o % HEAD + HEAD // 2) % HEAD, o] = 1.0

    L = {l: (lambda n, l=l: a[f"L{l}_xcond_{n}"]) for l in range(4)}
    z256 = zeros(FEAT, f32)
    d = {
        "x": a["x"], "ctx": a["ctx_1024"],
        "ctxt": a["ctx_1024"].transpose(2, 0, 1).reshape(KF, P, BATCH * CTX).transpose(1, 0, 2),
        "cond": a["cond_1024"].T.reshape(KF, P, BATCH).transpose(1, 0, 2),
        "mask_q": a["mask_SxS_bk0"], "mask_t": a["mask_SxS_bk0"].T,
        "kv_row": a["mask_BxS2_bf1"].reshape(1, BATCH * CTX),
        "kv_col": a["mask_BxS2_bf1"].T,
        "ident": np.eye(P, dtype=f32), "rotm": rot,
        "rope0": rope_table(512, 8).reshape(P, -1), "rope3": rope_table(1024, 8).reshape(P, -1),
        "mod_0": L[0]("adaLN_W"), "mod_1": L[1]("W_mod"), "mod_2": L[2]("w_ada"),
    }
    mod_bias = {0: L[0]("adaLN_b"), 1: L[1]("b_mod"), 2: L[2]("b_ada")}
    norm_w = {0: [L[0]("norm1_w"), L[0]("normc_w"), L[0]("norm2_w")]}
    mb, mw = [], []
    for l, i in NORMS:
        if l == 3:
            d[f"mod_{l}_{i}"] = L[3](f"ln{i + 1}_w").T
        for s in range(2):
            c = LAYERS[l]["norms"][i][s]
            bias = L[3](f"ln{i + 1}_b") if l == 3 else mod_bias[l]
            mb.append(cols(bias[c * FEAT:(c + 1) * FEAT]))
            mw.append(cols(norm_w[0][i]) if l == 0 and s == 0 else np.ones((P, KF), f32))
    d["modb"] = np.stack([np.concatenate(mb, 1), np.concatenate(mw, 1)], 1)

    cat = np.concatenate
    d.update({
        "qkv_0": L[0]("qkv_W"), "qkv_1": L[1]("W_qkv"), "qkv_2": L[2]("w_qkv"), "qkv_3": L[3]("qkv_w").T,
        "o_0": L[0]("attn_out_W"), "o_1": L[1]("W_proj"), "o_2": L[2]("w_so"), "o_3": L[3]("sa_out_w").T,
        "cq_0": L[0]("cq_W"), "cq_1": L[1]("W_qc"), "cq_2": L[2]("w_q"), "cq_3": L[3]("q_w").T,
        "ckv_0": cat([L[0]("ck_W"), L[0]("cv_W")], 1), "ckv_1": L[1]("W_kvc"), "ckv_2": L[2]("w_kv"),
        "ckv_3": cat([L[3]("k_w").T, L[3]("v_w").T], 1),
        "co_0": L[0]("co_W"), "co_1": L[1]("W_cproj"), "co_2": L[2]("w_co"), "co_3": L[3]("ca_out_w").T,
        "w1_0": L[0]("mlp_W1"), "w1_1": L[1]("W_mlp1"), "w1_2": L[2]("w_m1"), "w1_3": L[3]("ffn_w1").T,
        "w2_0": L[0]("mlp_W2"), "w2_1": L[1]("W_mlp2"), "w2_2": L[2]("w_m2"), "w2_3": L[3]("ffn_w2").T,
    })
    qkv_b = {1: L[1]("b_qkv"), 2: L[2]("b_qkv")}
    cq_b = {1: L[1]("b_qc"), 2: L[2]("b_q")}
    ckv_b = {1: L[1]("b_kvc"), 2: L[2]("b_kv")}
    b1 = {0: L[0]("mlp_b1"), 1: L[1]("b_mlp1"), 2: L[2]("b_m1"), 3: L[3]("ffn_b1")}
    out_b = {(0, 2): L[0]("mlp_b2"), (1, 0): L[1]("b_proj"), (1, 1): L[1]("b_cproj"), (1, 2): L[1]("b_mlp2"),
             (2, 0): L[2]("b_so"), (2, 1): L[2]("b_co"), (2, 2): L[2]("b_m2"), (3, 2): L[3]("ffn_b2")}
    table = zeros((P, 4, 24), f32)
    for l in range(4):
        if l in qkv_b:
            table[:, l, 0:4] = cols(qkv_b[l][0:2 * FEAT])
            table[:, l, 4:6] = cols(cq_b[l])
            table[:, l, 6:8] = cols(ckv_b[l][0:FEAT])
        table[:, l, 8:8 + len(b1[l]) // P] = cols(b1[l])
        for i in range(3):
            c = LAYERS[l]["gates"][i]
            d[f"gb_{l}_{i}"] = mod_bias[l][c * FEAT:(c + 1) * FEAT] if c is not None else z256
            d[f"ob_{l}_{i}"] = out_b.get((l, i), z256)
            d[f"vb_{l}_{i}"] = z256
        if l in qkv_b:
            d[f"vb_{l}_0"] = qkv_b[l][2 * FEAT:]
            d[f"vb_{l}_1"] = ckv_b[l][FEAT:]
    d["cols"] = table

    nc = bacc.Bacc("TRN2", target_bir_lowering=False, num_devices=1)
    arrays, aps = {}, {}
    for name, v in d.items():
        v = np.ascontiguousarray(v)
        arrays["in_" + name] = v
        aps[name] = nc.dram_tensor("in_" + name, v.shape, mybir.dt.from_np(v.dtype), kind="ExternalInput").ap()
    out = nc.dram_tensor("out_x", (BATCH, TOKENS, FEAT), mybir.dt.float32, kind="ExternalOutput").ap()
    blocks_kernel(nc, aps, out)
    r = run_bass_kernel_spmd(nc, [arrays], core_ids=[0])
    return r.results[0]["out_x"]
```
